# Optimizing a Trainium2 kernel written in Bass

```python
import numpy as np
import jax
import jax.numpy as jnp

def _softmax(x, axis=-1):
    return jax.nn.softmax(x, axis=axis)

def _gelu(x):
    return jax.nn.gelu(x, approximate=True)

def _silu(x):
    return jax.nn.silu(x)

def _sigmoid(x):
    return jax.nn.sigmoid(x)

def _layernorm(x, axis=-1, eps=1e-05):
    m = jnp.mean(x, axis=axis, keepdims=True)
    v = jnp.var(x, axis=axis, keepdims=True)
    return (x - m) / jnp.sqrt(v + eps)

def _scatter_add(tgt, idx, src, axis=0):
    return tgt.at[idx].add(src)

def _segment_sum(src, seg, n):
    return jax.ops.segment_sum(src, seg, n)
kernel_name = 'mk_prb_d1_jaxref_r8_01c802'

def setup_inputs(seed: int=0):
    np.random.seed(seed)
    _w = jnp.asarray

    def _L0_attn_setup():
        import jax, jax.numpy as jnp
        import numpy as np
        EMBED = 128
        H = 16
        KV = 4
        D = 64
        K_NODES = 4
        TOP_K = 2
        MAXLEN = 1024
        BASE = 10000.0
        SCALE = D ** (-0.5)
        NEG = -1000000000.0

        def _rotate_half(t):
            h = t.shape[-1] // 2
            return jnp.concatenate([-t[..., h:], t[..., :h]], axis=-1)

        def _rope_cache():
            inv_freq = 1.0 / BASE ** (jnp.arange(0, D, 2, dtype=jnp.float32) / D)
            t = jnp.arange(MAXLEN, dtype=jnp.float32)
            freqs = t[:, None] * inv_freq[None, :]
            emb = jnp.concatenate([freqs, freqs], axis=-1)
            return (jnp.cos(emb), jnp.sin(emb))
        key = jax.random.key(seed)
        ks = jax.random.split(key, 6)
        B, N = (1, 256)
        x = jax.random.normal(ks[0], (B, N, EMBED), jnp.float32)
        wq = 0.02 * jax.random.normal(ks[1], (EMBED, H * D), jnp.float32)
        wk = 0.02 * jax.random.normal(ks[2], (EMBED, KV * D), jnp.float32)
        wv = 0.02 * jax.random.normal(ks[3], (EMBED, KV * D), jnp.float32)
        wr = 0.02 * jax.random.normal(ks[4], (EMBED, H * K_NODES), jnp.float32)
        wo = 0.02 * jax.random.normal(ks[5], (H * D, EMBED), jnp.float32)
        return {'x': x, 'wq': wq, 'wk': wk, 'wv': wv, 'wr': wr, 'wo': wo}
    _L0_attn_in = _L0_attn_setup()

    def _L0_ffn_setup():
        import jax, jax.numpy as jnp
        import numpy as np
        D_MODEL = 128
        M = 64
        INNER = 16
        key = jax.random.key(seed)
        ks = jax.random.split(key, 9)

        def init(k, shape, fan_in):
            bound = 1.0 / np.sqrt(fan_in)
            return jax.random.uniform(k, shape, jnp.float32, -bound, bound)
        x = jax.random.normal(ks[0], (16, 512, D_MODEL), dtype=jnp.float32)
        Win = init(ks[1], (D_MODEL, M), D_MODEL)
        bin_ = init(ks[2], (M,), D_MODEL)
        W1 = init(ks[3], (M, INNER), 1)
        b1 = init(ks[4], (M, INNER), 1)
        W2 = init(ks[5], (M, INNER), INNER)
        b2 = init(ks[6], (M,), INNER)
        Wout = init(ks[7], (M, D_MODEL), M)
        bout = init(ks[8], (D_MODEL,), M)
        return {'x': x, 'Win': Win, 'bin_': bin_, 'W1': W1, 'b1': b1, 'W2': W2, 'b2': b2, 'Wout': Wout, 'bout': bout}
    _L0_ffn_in = _L0_ffn_setup()
    _d = {'L0_attn_x': _L0_attn_in['x'], 'L0_attn_wq': _L0_attn_in['wq'], 'L0_attn_wk': _L0_attn_in['wk'], 'L0_attn_wv': _L0_attn_in['wv'], 'L0_attn_wr': _L0_attn_in['wr'], 'L0_attn_wo': _L0_attn_in['wo'], 'L0_ffn_Win': _L0_ffn_in['Win'], 'L0_ffn_bin_': _L0_ffn_in['bin_'], 'L0_ffn_W1': _L0_ffn_in['W1'], 'L0_ffn_b1': _L0_ffn_in['b1'], 'L0_ffn_W2': _L0_ffn_in['W2'], 'L0_ffn_b2': _L0_ffn_in['b2'], 'L0_ffn_Wout': _L0_ffn_in['Wout'], 'L0_ffn_bout': _L0_ffn_in['bout']}
    _x0 = _d['L0_attn_x']
    _d['L0_attn_x'] = jax.random.normal(jax.random.fold_in(jax.random.key(seed), 1), (32, 256, 128), dtype=_x0.dtype)
    del _x0
    return _d

def reference(L0_attn_x, L0_attn_wq, L0_attn_wk, L0_attn_wv, L0_attn_wr, L0_attn_wo, L0_ffn_Win, L0_ffn_bin_, L0_ffn_W1, L0_ffn_b1, L0_ffn_W2, L0_ffn_b2, L0_ffn_Wout, L0_ffn_bout):

    def _L0_attn_ref(x, wq, wk, wv, wr, wo):
        import jax, jax.numpy as jnp
        import numpy as np
        EMBED = 128
        H = 16
        KV = 4
        D = 64
        K_NODES = 4
        TOP_K = 2
        MAXLEN = 1024
        BASE = 10000.0
        SCALE = D ** (-0.5)
        NEG = -1000000000.0

        def _rotate_half(t):
            h = t.shape[-1] // 2
            return jnp.concatenate([-t[..., h:], t[..., :h]], axis=-1)

        def _rope_cache():
            inv_freq = 1.0 / BASE ** (jnp.arange(0, D, 2, dtype=jnp.float32) / D)
            t = jnp.arange(MAXLEN, dtype=jnp.float32)
            freqs = t[:, None] * inv_freq[None, :]
            emb = jnp.concatenate([freqs, freqs], axis=-1)
            return (jnp.cos(emb), jnp.sin(emb))
        B, N, _ = x.shape
        G = H // KV
        q = (x @ wq).reshape(B, N, H, D).transpose(0, 2, 1, 3)
        k = (x @ wk).reshape(B, N, KV, D).transpose(0, 2, 1, 3)
        v = (x @ wv).reshape(B, N, KV, D).transpose(0, 2, 1, 3)
        k = jnp.repeat(k, G, axis=1)
        v = jnp.repeat(v, G, axis=1)
        logits = (x @ wr).reshape(B, N, H, K_NODES).transpose(0, 2, 1, 3)
        tk_vals, tk_idx = jax.lax.top_k(logits, TOP_K)
        tk_w = jax.nn.softmax(tk_vals, axis=-1)
        member = jax.nn.one_hot(tk_idx, K_NODES, dtype=jnp.float32).sum(axis=-2) > 0
        m_i = member.astype(jnp.int32)
        pos = jnp.cumsum(m_i, axis=2) - m_i
        cos_c, sin_c = _rope_cache()
        causal = jnp.tril(jnp.ones((N, N), dtype=bool))
        outs = []
        for n in range(K_NODES):
            p = pos[..., n]
            c = cos_c[p]
            s = sin_c[p]
            qr = q * c + _rotate_half(q) * s
            kr = k * c + _rotate_half(k) * s
            scores = jnp.einsum('bhid,bhjd->bhij', qr, kr) * SCALE
            mk = member[..., n][:, :, None, :]
            scores = jnp.where(causal[None, None] & mk, scores, NEG)
            probs = jax.nn.softmax(scores, axis=-1)
            outs.append(jnp.einsum('bhij,bhjd->bhid', probs, v))
        outs = jnp.stack(outs, axis=3)
        gathered = jnp.take_along_axis(outs, tk_idx[..., None], axis=3)
        y = (tk_w[..., None] * gathered).sum(axis=3)
        y = y.transpose(0, 2, 1, 3).reshape(B, N, H * D)
        return y @ wo

    def _L0_ffn_ref(x, Win, bin_, W1, b1, W2, b2, Wout, bout):
        import jax, jax.numpy as jnp
        import numpy as np
        D_MODEL = 128
        M = 64
        INNER = 16
        s = jnp.einsum('btd,dm->btm', x, Win) + bin_
        h = jax.nn.relu(s[..., None] * W1 + b1)
        g = jnp.einsum('btmh,mh->btm', h, W2) + b2
        out = jnp.einsum('btm,md->btd', g, Wout) + bout
        return out
    x = L0_attn_x
    xn = _layernorm(x, axis=-1)
    x = x + _L0_attn_ref(xn, L0_attn_wq, L0_attn_wk, L0_attn_wv, L0_attn_wr, L0_attn_wo) + _L0_ffn_ref(xn, L0_ffn_Win, L0_ffn_bin_, L0_ffn_W1, L0_ffn_b1, L0_ffn_W2, L0_ffn_b2, L0_ffn_Wout, L0_ffn_bout)
    return x

_drawn_inputs = setup_inputs


def setup_inputs(seed=0):
    import zlib

    import numpy as np

    out = dict(_drawn_inputs(seed))
    spreads = {}
    factors = {'L0_attn_wq': 8.0, 'L0_attn_wk': 8.0, 'L0_attn_wr': 4.713, 'L0_ffn_bin_': 8.0}
    for name, (base, spread) in spreads.items():
        noise = np.random.default_rng([zlib.crc32(name.encode()), seed]).standard_normal(out[name].shape)
        drawn = base * np.exp(spread * noise) if base else spread * noise
        out[name] = jnp.asarray(drawn.astype(out[name].dtype))
    for name, factor in factors.items():
        out[name] = (out[name] * factor).astype(out[name].dtype)
    return out
```

```python
import concourse.bass as bass
from concourse import mybir
from contextlib import ExitStack

import numpy as np

B, N, E = 32, 256, 128
NH, NKV, D, ND = 16, 4, 64, 4
HP = NH // 2
NB = N // 128
F = D // 2
M, INNER = 64, 16
SCALE = float(D) ** -0.5
BIG = 1.0e9
EPS = 1.0e-5
ROUND = 12582912.0
TURN = 6.283185
C_ID, C_TRI, C_BEFORE, C_FREQ, C_COLS = 0, 128, 256, 384, 385


def shape_constants():
    c = np.zeros((128, C_COLS), np.float32)
    row, col = np.arange(128)[:, None], np.arange(128)[None, :]
    c[:, C_ID:C_ID + 128] = row == col
    c[:, C_TRI:C_TRI + 128] = np.where(col > row, -BIG, 0.0)
    c[:, C_BEFORE:C_BEFORE + 128] = row < col
    freq = 1.0 / 10000.0 ** (np.arange(0, D, 2, dtype=np.float64) / D)
    c[:, C_FREQ] = (freq / (2 * np.pi)).astype(np.float32)[np.arange(128) % F]
    return c


def routed_attention_block(nc, x, wq, wk, wv, wr, wo, Win, bin_, W1, b1, W2, b2, Wout, bout, consts, out):
    fp32, bf16 = mybir.dt.float32, mybir.dt.bfloat16
    ALU, ACT, AX = mybir.AluOpType, mybir.ActivationFunctionType, mybir.AxisListType

    ctx = ExitStack()
    with ctx:
        def sb(name, shape, dt=fp32):
            return ctx.enter_context(nc.sbuf_tensor(name, shape, dt))

        def sem(name):
            return ctx.enter_context(nc.semaphore(name))

        cst = sb("cst", [128, C_COLS])
        ident = cst[:, C_ID:C_ID + 128]
        ident_bf = sb("ident_bf", [128, 128], bf16)
        before_bf = sb("before_bf", [128, 128], bf16)
        ones_bf = sb("ones_bf", [128, 128], bf16)
        causal0 = sb("causal0", [128, 2, 128])
        causal1 = sb("causal1", [128, 2, 256])
        quarter = sb("quarter", [128, 1])
        eps = sb("eps", [128, 1])
        wq_sb = sb("wq_sb", [128, NH * D])
        wq_rot = sb("wq_rot", [128, NH * D])
        wk_two = sb("wk_two", [128, NKV, 2, D])
        wk_rot = sb("wk_rot", [128, NKV, 2, D])
        wv_sb = sb("wv_sb", [128, NKV * D])
        wr_sb = sb("wr_sb", [128, NH * ND])
        wo_sb = sb("wo_sb", [128, HP, E])
        win_sb = sb("win_sb", [128, M])
        wout_sb = sb("wout_sb", [128, NB, E])
        bin_sb = sb("bin_sb", [128, 1])
        b2_sb = sb("b2_sb", [128, 1])
        w1_sb = sb("w1_sb", [128, INNER])
        b1_sb = sb("b1_sb", [128, INNER])
        w2_sb = sb("w2_sb", [128, INNER])
        bout_sb = sb("bout_sb", [128, E])
        mean = sb("mean", [128, B * NB])
        rstd = sb("rstd", [128, B * NB])
        va, vb, vc = (sb(n, [128, B * NB]) for n in ("va", "vb", "vc"))
        x_ln = sb("x_ln", [128, 2, NB, E])
        x_res = sb("x_res", [128, 2, NB, E])
        xn = sb("xn", [128, NB, E])
        xnT = sb("xnT", [128, 2, N])
        lg = sb("lg", [128, NB * NH, ND])
        ge0 = sb("ge0", [128, NB * NH, 3])
        ge1 = sb("ge1", [128, NB * NH, 2])
        ge2 = sb("ge2", [128, NB * NH, 1])
        win = sb("win", [128, NB * NH, ND])
        mem = sb("mem", [128, NB * NH, ND])
        mem_bf = sb("mem_bf", [128, NB * NH, ND], bf16)
        low = sb("low", [128, NB * NH, 1])
        slot = sb("slot", [128, 2, NB * NH, ND])
        sel = sb("sel", [128, NB * NH, 2, ND])
        sv = sb("sv", [128, NB * NH, 2])
        se = sb("se", [128, NB * NH, 2])
        smax = sb("smax", [128, NB * NH, 1])
        ssum = sb("ssum", [128, NB * NH, 1])
        wslot = sb("wslot", [128, 2, NB, NH, 2])
        pos_bf = sb("pos_bf", [128, NB * NH, 2], bf16)
        code = sb("code", [64, 2, 2, 2 * N])
        turns = sb("turns", [128, 2, 2 * N])
        whole = sb("whole", [128, 2, 2 * N])
        cs = sb("cs", [128, 2, HP, 2, 2 * N])
        prod = sb("prod", [128, 2, 2, 2 * N])
        rot = sb("rot", [128, 2, 2, 2 * N])
        qk = sb("qk", [128, 2, 2, 2, 2 * N])
        neg_s = sb("neg_s", [128, 2, 3, 512])
        neg_max = sb("neg_max", [128, 2, 4])
        expd = sb("expd", [128, 2, 3, 512])
        total = sb("total", [128, 2, 4])
        recip = sb("recip", [128, 2, 4])
        coef = sb("coef", [128, 2, 4])
        sums = sb("sums", [128, 2, 768])
        probs = sb("probs", [128, 2, 384])
        probsT = sb("probsT", [128, 2, 384])
        v_sb = sb("v_sb", [128, 2, NB, NKV * D])
        yT = sb("yT", [128, HP, N])
        sT = sb("sT", [128, 128])
        hT = sb("hT", [128, 4, 128])
        gT = sb("gT", [128, 2, 128])
        part = sb("part", [128, NB, E])
        res = sb("res", [128, 2, NB, E])

        wk_in = prod[:, 0, 0, 0:NKV * D]
        st = expd[:, 0, 0, 0:B * NB * 6].rearrange("p (t c) -> p t c", c=6)

        def pb(name):
            return ctx.enter_context(nc.psum_tensor(name, [128, 512], fp32))

        p_score = [pb(f"p_score{u}") for u in range(3)]
        p_q, p_k, p_misc, p_pt, p_y = (pb(n) for n in ("p_q", "p_k", "p_misc", "p_pt", "p_y"))

        consts_in, weights_in = sem("consts_in"), sem("weights_in")
        x_all_in, norm_step, std_ready = sem("x_all_in"), sem("norm_step"), sem("std_ready")
        norm_sync, weights_made, consts_made = sem("norm_sync"), sem("weights_made"), sem("consts_made")
        zeroed, stats_read = sem("zeroed"), sem("stats_read")
        x_ln_in = [sem("x_ln_in0"), sem("x_ln_in1")]
        x_res_in = [sem("x_res_in0"), sem("x_res_in1")]
        stored = [sem("stored0"), sem("stored1")]
        xn_made, xnT_mm, xnT_made = sem("xn_made"), sem("xnT_mm"), sem("xnT_made")
        logits_mm, logits_made, sT_made = sem("logits_mm"), sem("logits_made"), sem("sT_made")
        route_step, mem_made, slot_made, slot_exp = sem("route_step"), sem("mem_made"), sem("slot_made"), sem("slot_exp")
        diff_made, wslot_made = sem("diff_made"), sem("wslot_made")
        pos_mm, pos_sel, pos_made = sem("pos_mm"), sem("pos_sel"), sem("pos_made")
        code_mm, code_made = sem("code_mm"), sem("code_made")
        v_mm, v_made = sem("v_mm"), sem("v_made")
        turn_mm, turn_made, whole_made = sem("turn_mm"), sem("turn_made"), sem("whole_made")
        frac_made, abs_made, table_made = sem("frac_made"), sem("abs_made"), sem("table_made")
        q_mm, k_mm, q_prod, k_prod = sem("q_mm"), sem("k_mm"), sem("q_prod"), sem("k_prod")
        rot_made = sem("rot_made")
        qk_in = [sem("qk_in0"), sem("qk_in1")]
        score_mm, score_neg, exp_made, slots_added = sem("score_mm"), sem("score_neg"), sem("exp_made"), sem("slots_added")
        coef_step, probs_made, pt_mm, pt_made = sem("coef_step"), sem("probs_made"), sem("pt_mm"), sem("pt_made")
        y_mm, yT_made = sem("y_mm"), sem("yT_made")
        relu_made, g_step = sem("relu_made"), sem("g_step")
        pe_waited, dve_waited = sem("pe_waited"), sem("dve_waited")
        out_mm, out_read, out_made = sem("out_mm"), sem("out_read"), sem("out_made")

        WEIGHT_LOADS = 7 + 6 * NB

        x_tok = x.rearrange("b (n p) e -> p b n e", p=128)
        out_tok = out.rearrange("b (n p) e -> p b n e", p=128)

        def wait(eng, s, value):
            if not (isinstance(value, int) and value <= 0):
                eng.wait_ge(s, value)

        def first(b):
            return isinstance(b, int) and b == 0

        def loads_of(b, par):
            return b * 8 + (16 - 8 * par)

        def body(eng, steps, prologue):
            prologue()
            steps(0, 0, True)
            with eng.Fori(0, (B - 2) // 2) as i:
                steps(i * 2 + 1, 1, True)
                steps(i * 2 + 2, 0, True)
            steps(B - 1, 1, False)

        def lagged(b, k, lag):
            g = k - lag
            if g < 0:
                return b - 1, g + NH, not first(b)
            return b, g, g < NH

        block = ctx.enter_context(nc.Block())

        @block.sync
        def _(sp):
            def load_ln(nb, par):
                wait(sp, xn_made, nb - 1)
                sp.dma_start(x_ln[:, par], x_tok[:, bass.ds(nb, 1)]).then_inc(x_ln_in[par], 16)

            def place(b, hp, par):
                H, r = b * HP + hp, hp % 2
                wait(sp, rot_made, 2 * H + 2)
                wait(sp, score_mm, 6 * H - 6)
                if hp == 0:
                    sp.wait_ge(code_made, 2 * b + 2)
                for h in range(2):
                    sp.dma_start(qk[64 * h:64 * h + 64, r, :, h, :], rot[64 * h:64 * h + 64, r]).then_inc(qk_in[r], 16)
                    head = 2 * hp + h
                    c0 = 64 - 64 * h
                    sp.dma_start(qk[c0:c0 + ND, r, :, h, :], code[ND * head:ND * head + ND, par]).then_inc(qk_in[r], 16)

            def prologue():
                sp.dma_start(cst[:, :], consts).then_inc(consts_in, 16)
                stage = cs[:, 1].rearrange("p a b c -> p (a b c)").rearrange("p (t n e) -> p t n e", t=B, n=NB)
                for q in range(4):
                    sp.dma_start(stage[:, 8 * q:8 * q + 8], x_tok[:, 8 * q:8 * q + 8]).then_inc(x_all_in, 16)
                sp.dma_start(wq_sb[:, :], wq).then_inc(weights_in, 16)
                sp.dma_start(wk_in, wk).then_inc(weights_in, 16)
                sp.dma_start(wv_sb[:, :], wv).then_inc(weights_in, 16)
                sp.dma_start(wr_sb[:, :], wr).then_inc(weights_in, 16)
                sp.dma_start(wo_sb[:, :, :], wo.rearrange("(h p) e -> p h e", p=128)).then_inc(weights_in, 16)
                sp.dma_start(win_sb[:, :], Win).then_inc(weights_in, 16)
                sp.dma_start(bout_sb[:, :], bout.rearrange("(o e) -> o e", o=1).broadcast_to([128, E])).then_inc(weights_in, 16)
                col = lambda v: v.rearrange("(m o) -> m o", o=1)
                for blk in range(NB):
                    rows = slice(64 * blk, 64 * blk + 64)
                    for dst, src in ((w1_sb, W1), (b1_sb, b1), (w2_sb, W2)):
                        sp.dma_start(dst[rows, :], src).then_inc(weights_in, 16)
                    sp.dma_start(bin_sb[rows, :], col(bin_)).then_inc(weights_in, 16)
                    sp.dma_start(b2_sb[rows, :], col(b2)).then_inc(weights_in, 16)
                load_ln(0, 0)
                sp.dma_start(x_res[:, 0], x_tok[:, 0:1]).then_inc(x_res_in[0], 16)
                sp.wait_ge(zeroed, 2)
                for blk in range(NB):
                    sp.dma_start(wout_sb[64 * blk:64 * blk + 64, blk, :], Wout).then_inc(weights_in, 16)
                place(0, 0, 0)

            def steps(b, par, more):
                for k in range(NH):
                    if k == 0 and more:
                        load_ln(b + 1, 1 - par)
                    if k == 6:
                        if not first(b):
                            sp.wait_ge(out_made, b)
                            sp.dma_start(out_tok[:, bass.ds(b - 1, 1)], res[:, 1 - par]).then_inc(stored[1 - par], 16)
                        if more:
                            if not first(b):
                                sp.wait_ge(stored[1 - par], loads_of(b - 1, 1 - par))
                            sp.dma_start(x_res[:, 1 - par], x_tok[:, bass.ds(b + 1, 1)]).then_inc(x_res_in[1 - par], 16)
                    if k % 2 == 0 and k < NH - 2:
                        place(b, k // 2 + 1, par)
                    if k == NH - 2 and more:
                        place(b + 1, 0, 1 - par)

            body(sp, steps, prologue)
            sp.wait_ge(out_made, B)
            sp.dma_start(out_tok[:, B - 1:B], res[:, (B - 1) % 2]).then_inc(stored[(B - 1) % 2], 16)
            sp.wait_ge(stored[0], 16 * (B // 2))
            sp.wait_ge(stored[1], 16 * (B // 2))

        @block.tensor
        def _(pe):
            mm = nc.tensor.matmul

            def transpose_x(nb, par):
                pe.wait_ge(xn_made, nb + 1)
                wait(pe, turn_made, HP * nb)
                for blk in range(NB):
                    last = nc.tensor.transpose(p_misc[:, 128 * blk:128 * blk + 128], xn[:, blk, :], ident)
                last.then_inc(xnT_mm, 1)

            def logits(nb, par):
                pe.wait_ge(xnT_made, nb + 1)
                for blk in range(NB):
                    mm(p_misc[:, 64 * blk:64 * blk + 64], xnT[:, par, 128 * blk:128 * blk + 128], wr_sb[:, :],
                       start=True, stop=True)
                for blk in range(NB):
                    last = mm(p_misc[64 * blk:64 * blk + 64, 128:256], win_sb[:, :],
                              xnT[:, par, 128 * blk:128 * blk + 128], start=True, stop=True)
                last.then_inc(logits_mm, 1)

            def values(nb, par):
                pe.wait_ge(logits_made, nb + 1)
                pe.wait_ge(sT_made, nb + 1)
                wait(pe, out_read, nb - 1)
                for blk in range(NB):
                    last = mm(p_misc[:, 256 * blk:256 * blk + 256], xnT[:, par, 128 * blk:128 * blk + 128],
                              wv_sb[:, :], start=True, stop=True)
                last.then_inc(v_mm, 1)

            def positions(nb, par):
                pe.wait_ge(mem_made, nb + 1)
                pe.wait_ge(v_made, nb + 1)
                m = mem_bf[:, :, :].rearrange("p (n h) d -> p n (h d)", n=NB)
                mm(p_misc[:, 0:64], before_bf[:, :], m[:, 0], start=True, stop=True)
                mm(p_misc[:, 64:128], ones_bf[:, :], m[:, 0], start=True, stop=False)
                mm(p_misc[:, 64:128], before_bf[:, :], m[:, 1], start=False, stop=True).then_inc(pos_mm, 1)

            def codes(nb, par):
                pe.wait_ge(slot_made, nb + 1)
                pe.wait_ge(pos_sel, nb + 1)
                pe.sem_inc(pe_waited, 1)
                for s in range(2):
                    for blk in range(NB):
                        at = 256 * s + 128 * blk
                        last = nc.tensor.transpose(p_misc[0:64, at:at + 128], slot[:, s, NH * blk:NH * blk + NH, :].rearrange("p h d -> p (h d)"), ident)
                last.then_inc(code_mm, 1)

            def turn(nb, hp):
                if hp == 0:
                    pe.wait_ge(pos_made, nb + 1)
                    pe.wait_ge(code_made, 2 * nb + 2)
                wait(pe, turn_made, HP * nb + hp)
                for s in range(2):
                    for blk in range(NB):
                        at = 256 * s + 128 * blk
                        for h in range(2):
                            one = pos_bf[:, NH * blk + 2 * hp + h, s:s + 1].broadcast_to([128, D])
                            last = mm(p_misc[64 * h:64 * h + 64, at:at + 128], one, ident_bf[:, :], start=True, stop=True)
                last.then_inc(turn_mm, 1)

            def project(b, hp, par):
                H = b * HP + hp
                pe.wait_ge(xnT_made, b + 1)
                wait(pe, q_prod, H)
                mm(p_q[:, 0:256], wq_sb[:, 128 * hp:128 * hp + 128], xnT[:, par], start=True, stop=True)
                mm(p_q[:, 256:512], wq_rot[:, 128 * hp:128 * hp + 128], xnT[:, par], start=True, stop=True).then_inc(q_mm, 1)
                if hp % 2 == 0:
                    wait(pe, k_prod, H)
                    kv = hp // 2
                    mm(p_k[:, 0:256], wk_two[:, kv].rearrange("p a d -> p (a d)"), xnT[:, par], start=True, stop=True)
                    mm(p_k[:, 256:512], wk_rot[:, kv].rearrange("p a d -> p (a d)"), xnT[:, par],
                       start=True, stop=True).then_inc(k_mm, 1)

            def scores(b, g):
                G, h, r = b * NH + g, g % 2, (g // 2) % 2
                H_in_ring = b * (HP // 2) + g // 4
                if h == 0:
                    pe.wait_ge(qk_in[r], 64 * H_in_ring + 64)
                q, key = qk[:, r, 0, h, :], qk[:, r, 1, h, :].rearrange("p (t j) -> p t j", t=2)
                wait(pe, score_neg, 3 * G - 2)
                for s in range(2):
                    last = mm(p_score[0][:, 256 * s:256 * s + 256], q[:, 256 * s:256 * s + 128], key[:, :, 0:128],
                              start=True, stop=True)
                last.then_inc(score_mm, 1)
                for s in range(2):
                    wait(pe, score_neg, 3 * G - 1 + s)
                    mm(p_score[1 + s][:, :], q[:, 256 * s + 128:256 * s + 256], key, start=True, stop=True).then_inc(score_mm, 1)

            def transpose_probs(b, g):
                G = b * NH + g
                pe.wait_ge(probs_made, G + 1)
                wait(pe, pt_made, G)
                for j in range(3):
                    last = nc.tensor.transpose(p_pt[:, 128 * j:128 * j + 128], probs[:, g % 2, 128 * j:128 * j + 128], ident)
                last.then_inc(pt_mm, 1)

            def mix_values(b, g, par):
                G, h, kv = b * NH + g, g % 2, g // (NH // NKV)
                pe.wait_ge(pt_made, G + 1)
                pe.wait_ge(v_made, b + 1)
                if h == 0:
                    wait(pe, yT_made, b * HP + g // 2)
                rows, vs = slice(64 * h, 64 * h + 64), slice(D * kv, D * kv + D)
                mm(p_y[rows, 0:256], v_sb[:, par, 0, vs], probsT[:, g % 2, 0:256], start=True, stop=False)
                mm(p_y[rows, 128:256], v_sb[:, par, 1, vs], probsT[:, g % 2, 256:384], start=False, stop=True).then_inc(y_mm, 1)

            def project_out(b, par, *bank_read):
                for s, value in bank_read:
                    pe.wait_ge(s, value)
                pe.wait_ge(yT_made, HP * b + HP)
                pe.wait_ge(g_step, INNER * (b + 1))
                for blk in range(NB):
                    o = p_misc[:, 128 * blk:128 * blk + 128]
                    for hp in range(HP):
                        mm(o, yT[:, hp, 128 * blk:128 * blk + 128], wo_sb[:, hp, :], start=(hp == 0), stop=False)
                    last = mm(o, gT[:, par, :], wout_sb[:, blk, :], start=False, stop=True)
                last.then_inc(out_mm, 1)

            def prologue():
                pe.wait_ge(consts_in, 16)
                pe.wait_ge(consts_made, 3)
                pe.wait_ge(weights_in, 16 * WEIGHT_LOADS)
                pe.wait_ge(weights_made, 5)
                transpose_x(0, 0)
                logits(0, 0)
                values(0, 0)
                positions(0, 0)
                codes(0, 0)
                for hp in range(HP):
                    turn(0, hp)
                project(0, 0, 0)
                project(0, 1, 0)

            def steps(b, par, more):
                for k in range(NH + (0 if more else 3)):
                    if k < NH:
                        scores(b, k)
                    lb, g, there = lagged(b, k, 2)
                    if there:
                        transpose_probs(lb, g)
                    lb, g, there = lagged(b, k, 3)
                    if there:
                        mix_values(lb, g, par if k >= 3 else 1 - par)
                    if k < NH and k % 2 == 1:
                        hp = (k + 3) // 2
                        if hp < HP:
                            project(b, hp, par)
                        elif more:
                            project(b + 1, hp - HP, 1 - par)
                    if more and k == 0:
                        transpose_x(b + 1, 1 - par)
                    if more and k == 1:
                        logits(b + 1, 1 - par)
                    if k == 3 and not first(b):
                        project_out(b - 1, 1 - par, *(((logits_made, b + 2), (sT_made, b + 2)) if more else ((turn_made, HP * B),)))
                    if more and k == 3:
                        values(b + 1, 1 - par)
                        positions(b + 1, 1 - par)
                    if more and k == 5:
                        codes(b + 1, 1 - par)
                    if more and 6 <= k < 10:
                        turn(b + 1, 2 * (k - 6))
                        turn(b + 1, 2 * (k - 6) + 1)

            body(pe, steps, prologue)
            project_out(B - 1, (B - 1) % 2, (out_read, B - 1))

        @block.scalar
        def _(act):
            fn = nc.scalar.activation

            def keep_xT(nb, par):
                act.wait_ge(xnT_mm, nb + 1)
                wait(act, q_mm, HP * (nb - 1))
                fn(xnT[:, par], p_misc[:, 0:256], ACT.Copy).then_inc(xnT_made, 1)

            def keep_logits(nb):
                act.wait_ge(logits_mm, nb + 1)
                wait(act, wslot_made, nb)
                wait(act, relu_made, INNER * nb)
                fn(lg[:, :, :].rearrange("p a d -> p (a d)"), p_misc[:, 0:128], ACT.Copy).then_inc(logits_made, 1)
                fn(sT[:, :], p_misc[:, 128:256], ACT.Identity, bias=bin_sb[:, 0:1]).then_inc(sT_made, 1)

            def keep_values(nb, par):
                act.wait_ge(v_mm, nb + 1)
                wait(act, y_mm, NH * (nb - 1))
                fn(v_sb[:, par].rearrange("p n d -> p (n d)"), p_misc[:, :], ACT.Copy).then_inc(v_made, 1)

            def slot_exps(nb):
                act.wait_ge(diff_made, nb + 1)
                wait(act, wslot_made, nb)
                fn(se[:, :, :], sv[:, :, :], ACT.Exp).then_inc(slot_exp, 1)

            def keep_codes(nb, par):
                act.wait_ge(code_mm, nb + 1)
                for r in range(2):
                    wait(act, qk_in[r], 64 * (HP // 2) * (nb - 1))
                fn(code[:, par, 0, :], p_misc[0:64, :], ACT.Copy, scale=-1.0, bias=1.0).then_inc(code_made, 1)
                fn(code[:, par, 1, :], p_misc[0:64, :], ACT.Copy, scale=-BIG).then_inc(code_made, 1)

            def keep_turns(nb, hp):
                act.wait_ge(turn_mm, HP * nb + hp + 1)
                wait(act, frac_made, HP * nb + hp - 1)
                fn(turns[:, hp % 2], p_misc[:, :], ACT.Copy, scale=cst[:, C_FREQ:C_FREQ + 1]).then_inc(turn_made, 1)

            def trig(nb, par):
                act.wait_ge(abs_made, HP * (nb + 1))
                act.wait_ge(frac_made, HP * (nb + 1))
                cos, sin = cs[:, par, :, 0, :], cs[:, par, :, 1, :]
                fn(cos, cos, ACT.Sin, bias=quarter[:, 0:1], scale=-TURN).then_inc(table_made, 1)
                fn(sin, sin, ACT.Sin, scale=TURN).then_inc(table_made, 1)

            def relus(nb, js):
                for j in js:
                    act.wait_ge(sT_made, nb + 1)
                    wait(act, g_step, INNER * nb + j - 3)
                    fn(hT[:, j % 4], sT[:, :], ACT.Relu, bias=b1_sb[:, j:j + 1], scale=w1_sb[:, j:j + 1]).then_inc(relu_made, 1)

            def exps(b, g):
                G, r = b * NH + g, g % 2
                act.wait_ge(score_neg, 3 * G + 1)
                wait(act, slots_added, 2 * G - 3)
                wait(act, probs_made, G - 1)
                for s in range(2):
                    last = fn(expd[:, r, 0, 256 * s:256 * s + 256], neg_s[:, r, 0, 256 * s:256 * s + 256], ACT.Exp,
                              bias=neg_max[:, r, s:s + 1], scale=-1.0, accum_out=total[:, r, s:s + 1])
                last.then_inc(exp_made, 1)
                wait(act, slots_added, 2 * G - 2)
                for s in range(2):
                    act.wait_ge(score_neg, 3 * G + 2 + s)
                    fn(expd[:, r, 1 + s, :], neg_s[:, r, 1 + s, :], ACT.Exp, bias=neg_max[:, r, 2 + s:3 + s], scale=-1.0,
                       accum_out=total[:, r, 2 + s:3 + s]).then_inc(exp_made, 1)

            def keep_probsT(b, g):
                G = b * NH + g
                act.wait_ge(pt_mm, G + 1)
                wait(act, y_mm, G - 1)
                fn(probsT[:, g % 2], p_pt[:, 0:384], ACT.Copy).then_inc(pt_made, 1)

            def keep_yT(b, hp):
                act.wait_ge(y_mm, 2 * (b * HP + hp) + 2)
                if hp == 0:
                    wait(act, out_mm, b)
                fn(yT[:, hp], p_y[:, 0:256], ACT.Copy).then_inc(yT_made, 1)

            def prologue():
                act.wait_ge(norm_sync, 1)
                fn(vc[:, :], vb[:, :], ACT.Sqrt, bias=eps[:, 0:1]).then_inc(std_ready, 1)
                keep_xT(0, 0)
                keep_logits(0)
                keep_values(0, 0)
                slot_exps(0)
                keep_codes(0, 0)
                for hp in range(HP):
                    keep_turns(0, hp)
                trig(0, 0)
                relus(0, range(INNER))

            def steps(b, par, more):
                for k in range(NH + (0 if more else 3)):
                    lb, g, there = lagged(b, k, 1)
                    if there:
                        exps(lb, g)
                    lb, g, there = lagged(b, k, 2)
                    if there:
                        keep_probsT(lb, g)
                    lb, g, there = lagged(b, k, 3)
                    if there and g % 2 == 1:
                        keep_yT(lb, g // 2)
                    if not more:
                        continue
                    if k == 0:
                        keep_xT(b + 1, 1 - par)
                    if k == 1:
                        keep_logits(b + 1)
                    if k == 3:
                        keep_values(b + 1, 1 - par)
                        slot_exps(b + 1)
                    if k == 5:
                        keep_codes(b + 1, 1 - par)
                    if 6 <= k < 10:
                        keep_turns(b + 1, 2 * (k - 6))
                        keep_turns(b + 1, 2 * (k - 6) + 1)
                    if k == 11:
                        trig(b + 1, 1 - par)
                    if 12 <= k:
                        relus(b + 1, range(4 * (k - 12), 4 * (k - 12) + 4))

            body(act, steps, prologue)

        @block.vector
        def _(dve):
            tt, ts, stt = nc.vector.tensor_tensor, nc.vector.tensor_scalar, nc.vector.scalar_tensor_tensor
            lgv = lg[:, :, :]

            def norm(nb, par):
                dve.wait_ge(x_ln_in[par], loads_of(nb, par))
                wait(dve, xnT_mm, nb)
                for blk in range(NB):
                    t = nb * NB + blk
                    last = ts(xn[:, blk, :], x_ln[:, par, blk, :], mean[:, bass.ds(t, 1)], rstd[:, bass.ds(t, 1)],
                              ALU.subtract, ALU.mult)
                last.then_inc(xn_made, 1)

            def route(nb, par, part):
                STEPS = 12
                count = [0 if part == 0 else 10]

                def step(ins):
                    count[0] += 1
                    ins.then_inc(route_step, 1)
                    dve.wait_ge(route_step, nb * STEPS + count[0])

                if part == 0:
                    dve.wait_ge(logits_made, nb + 1)
                    wait(dve, pos_mm, nb)
                    wait(dve, code_mm, nb)
                    l = lambda a, b_: lgv[:, :, a:b_]
                    tt(ge0[:, :, :], l(0, 1).broadcast_to([128, NB * NH, 3]), l(1, 4), ALU.is_ge)
                    tt(ge1[:, :, :], l(1, 2).broadcast_to([128, NB * NH, 2]), l(2, 4), ALU.is_ge)
                    step(tt(ge2[:, :, :], l(2, 3), l(3, 4), ALU.is_ge))
                    tt(win[:, :, 0:1], ge0[:, :, 0:1], ge0[:, :, 1:2], ALU.add)
                    tt(win[:, :, 1:2], ge1[:, :, 0:1], ge1[:, :, 1:2], ALU.add)
                    step(tt(win[:, :, 2:4], ge0[:, :, 1:3], ge1[:, :, :], ALU.add))
                    tt(win[:, :, 0:1], win[:, :, 0:1], ge0[:, :, 2:3], ALU.add)
                    tt(win[:, :, 1:2], win[:, :, 1:2], ge0[:, :, 0:1], ALU.subtract)
                    tt(win[:, :, 2:3], win[:, :, 2:3], ge2[:, :, :], ALU.subtract)
                    step(tt(win[:, :, 3:4], win[:, :, 3:4], ge2[:, :, :], ALU.add))
                    for n, (op, bound) in enumerate(((ALU.is_ge, 2.0), (ALU.is_ge, 1.0), (ALU.is_le, 0.0), (ALU.is_le, 1.0))):
                        last = ts(mem[:, :, n:n + 1], win[:, :, n:n + 1], bound, None, op)
                    step(last)
                    nc.vector.tensor_copy(mem_bf[:, :, :], mem[:, :, :]).then_inc(mem_made, 1)
                    nc.vector.tensor_copy(slot[:, 0, :, 0:1], mem[:, :, 0:1])
                    tt(slot[:, 0, :, 1:2], mem[:, :, 1:2], mem[:, :, 0:1], ALU.is_gt)
                    step(tt(low[:, :, :], mem[:, :, 0:1], mem[:, :, 1:2], ALU.add))
                    step(tt(slot[:, 0, :, 2:3], mem[:, :, 2:3], low[:, :, :], ALU.is_gt))
                    step(tt(slot[:, 1], mem[:, :, :], slot[:, 0], ALU.subtract))
                    ins = tt(sel[:, :, 0, :], slot[:, 0], lgv, ALU.mult)
                    ins.then_inc(slot_made, 1)
                    step(tt(sel[:, :, 1, :], slot[:, 1], lgv, ALU.mult))
                    step(nc.vector.tensor_reduce(sv[:, :, :], sel[:, :, :, :], AX.X, ALU.add))
                    step(tt(smax[:, :, :], sv[:, :, 0:1], sv[:, :, 1:2], ALU.max))
                    assert count[0] == 10
                    tt(sv[:, :, :], sv[:, :, :], smax[:, :, :].broadcast_to([128, NB * NH, 2]), ALU.subtract).then_inc(diff_made, 1)
                else:
                    dve.wait_ge(slot_exp, nb + 1)
                    step(tt(ssum[:, :, :], se[:, :, 0:1], se[:, :, 1:2], ALU.add))
                    step(nc.vector.reciprocal(ssum[:, :, :], ssum[:, :, :]))
                    w = wslot[:, par].rearrange("p n h s -> p (n h) s")
                    tt(w, se[:, :, :], ssum[:, :, :].broadcast_to([128, NB * NH, 2]), ALU.mult).then_inc(wslot_made, 1)
                    dve.wait_ge(pos_mm, nb + 1)
                    pos = p_misc[:, 0:128].rearrange("p (a d) -> p a d", d=ND)
                    tt(sel[:, :, 0, :], pos, slot[:, 0], ALU.mult)
                    tt(sel[:, :, 1, :], pos, slot[:, 1], ALU.mult).then_inc(pos_sel, 1)
                    dve.wait_ge(pos_sel, nb + 1)
                    with nc.allow_low_precision(reason="positions are integers below 256, exact in bf16"):
                        nc.vector.tensor_reduce(pos_bf[:, :, :], sel[:, :, :, :], AX.X, ALU.add).then_inc(pos_made, 1)

            def rounds(nb, hp):
                dve.wait_ge(turn_made, HP * nb + hp + 1)
                wait(dve, frac_made, HP * nb + hp - 1)
                ts(whole[:, hp % 2], turns[:, hp % 2], ROUND, -ROUND, ALU.add, ALU.add).then_inc(whole_made, 1)

            def absolutes(nb, par, hp):
                dve.wait_ge(frac_made, HP * nb + hp + 1)
                stt(cs[:, par, hp, 0, :], cs[:, par, hp, 1, :], -1.0, cs[:, par, hp, 1, :], ALU.mult, ALU.max).then_inc(abs_made, 1)

            def rotate(b, hp, par):
                H = b * HP + hp
                dve.wait_ge(table_made, 2 * b + 2)
                table = cs[:, par, hp].rearrange("p c (s i) -> p c s i", s=2)
                for what, (bank, mm_done, n, prod_done) in enumerate(((p_q, q_mm, H + 1, q_prod),
                                                                      (p_k, k_mm, b * (HP // 2) + hp // 2 + 1, k_prod))):
                    dve.wait_ge(mm_done, n)
                    wait(dve, rot_made, 2 * H - 1 + what)
                    for c in range(2):
                        last = tt(prod[:, what, c].rearrange("p (s i) -> p s i", s=2),
                                  bank[:, 256 * c:256 * c + 256].rearrange("p (o i) -> p o i", o=1).broadcast_to([128, 2, N]),
                                  table[:, c], ALU.mult)
                    last.then_inc(prod_done, 1)

            def negate(b, g):
                G, r = b * NH + g, g % 2
                ttr = nc.vector.tensor_tensor_reduce
                dve.wait_ge(score_mm, 3 * G + 1)
                wait(dve, exp_made, 3 * G - 5)
                dve.sem_inc(dve_waited, 1)
                for s in range(2):
                    cols = slice(256 * s, 256 * s + 256)
                    last = ttr(out=neg_s[:, r, 0, cols], in0=p_score[0][:, cols], in1=causal0[:, :, :].rearrange("p t j -> p (t j)"),
                               scale=-SCALE, scalar=3.0e38, op0=ALU.add, op1=ALU.min, accum_out=neg_max[:, r, s:s + 1])
                last.then_inc(score_neg, 1)
                for s in range(2):
                    dve.wait_ge(score_mm, 3 * G + 2 + s)
                    wait(dve, exp_made, 3 * G - 4 + s)
                    dve.sem_inc(dve_waited, 1)
                    ttr(out=neg_s[:, r, 1 + s, :], in0=p_score[1 + s][:, :], in1=causal1[:, :, :].rearrange("p t j -> p (t j)"),
                        scale=-SCALE, scalar=3.0e38, op0=ALU.add, op1=ALU.min,
                        accum_out=neg_max[:, r, 2 + s:3 + s]).then_inc(score_neg, 1)

            def combine(b, g, par):
                G, r = b * NH + g, g % 2
                dve.wait_ge(exp_made, 3 * G + 3)
                nc.vector.reciprocal(recip[:, r], total[:, r]).then_inc(coef_step, 1)
                dve.wait_ge(coef_step, 4 * G + 1)
                tt(coef[:, r].rearrange("p (n s) -> p n s", n=NB), wslot[:, par, :, g, :],
                   recip[:, r].rearrange("p (n s) -> p n s", n=NB), ALU.mult).then_inc(coef_step, 1)
                dve.wait_ge(coef_step, 4 * G + 2)
                dve.wait_ge(slots_added, 2 * G + 2)
                wait(dve, pt_mm, G - 1)
                p0, p1 = probs[:, r, 0:128], probs[:, r, 128:384]
                ts(p0, sums[:, r, 0:128], coef[:, r, 0:1], None, ALU.mult).then_inc(coef_step, 1)
                ts(p1, sums[:, r, 256:512], coef[:, r, 2:3], None, ALU.mult).then_inc(coef_step, 1)
                dve.wait_ge(coef_step, 4 * G + 3)
                stt(p0, sums[:, r, 128:256], coef[:, r, 1:2], p0, ALU.mult, ALU.add)
                dve.wait_ge(coef_step, 4 * G + 4)
                stt(p1, sums[:, r, 512:768], coef[:, r, 3:4], p1, ALU.mult, ALU.add).then_inc(probs_made, 1)

            def gate(nb, par, js):
                for j in js:
                    dve.wait_ge(relu_made, INNER * nb + j + 1)
                    if j == 0:
                        wait(dve, out_mm, nb - 1)
                        ts(gT[:, par], hT[:, 0], w2_sb[:, 0:1], b2_sb[:, 0:1], ALU.mult, ALU.add).then_inc(g_step, 1)
                    else:
                        dve.wait_ge(g_step, INNER * nb + j)
                        stt(gT[:, par], hT[:, j % 4], w2_sb[:, j:j + 1], gT[:, par], ALU.mult, ALU.add).then_inc(g_step, 1)

            def finish(b, par):
                dve.wait_ge(out_mm, b + 1)
                dve.wait_ge(x_res_in[par], loads_of(b, par))
                tt(part[:, :, :], p_misc[:, 0:256].rearrange("p (n e) -> p n e", n=NB), x_res[:, par], ALU.add).then_inc(out_read, 1)
                dve.wait_ge(out_read, b + 1)
                for blk in range(NB):
                    last = tt(res[:, par, blk, :], part[:, blk, :], bout_sb[:, :], ALU.add)
                last.then_inc(out_made, 1)

            def prologue():
                dve.wait_ge(consts_in, 16)
                for dst, src in ((ident_bf, ident), (before_bf, cst[:, C_BEFORE:C_BEFORE + 128])):
                    nc.vector.tensor_copy(dst[:, :], src).then_inc(consts_made, 1)
                nc.vector.memset(ones_bf[:, :], 1.0).then_inc(consts_made, 1)
                nc.vector.memset(quarter[:, :], float(np.pi / 2))
                nc.vector.memset(eps[:, :], EPS)
                nc.vector.memset(causal1[:, :, 0:128], 0.0)
                nc.vector.memset(slot[:, :, :, :], 0.0)
                tri = cst[:, C_TRI:C_TRI + 128]
                for t in range(2):
                    nc.vector.tensor_copy(causal0[:, t], tri)
                    nc.vector.tensor_copy(causal1[:, t, 128:256], tri)
                dve.wait_ge(x_all_in, 64)
                stage = cs[:, 1].rearrange("p a b c -> p (a b c)")
                with dve.Fori(0, B * NB // 8) as i:
                    for t in range(8):
                        tile = i * 8 + t
                        nc.vector.bn_stats(st[:, bass.ds(tile, 1), :].rearrange("p a b -> p (a b)"),
                                           stage[:, bass.ds(tile * 128, 128)]).then_inc(stats_read, 1)
                dve.wait_ge(stats_read, B * NB)
                c = [0]

                def step(ins):
                    c[0] += 1
                    ins.then_inc(norm_step, 1)
                    dve.wait_ge(norm_step, c[0])

                me, m2e, mo, m2o = st[:, :, 1], st[:, :, 2], st[:, :, 4], st[:, :, 5]
                tt(va[:, :], me, mo, ALU.subtract)
                step(tt(vb[:, :], m2e, m2o, ALU.add))
                step(tt(va[:, :], va[:, :], va[:, :], ALU.mult))
                step(tt(mean[:, :], me, mo, ALU.add))
                step(ts(mean[:, :], mean[:, :], 0.5, None, ALU.mult))
                step(stt(va[:, :], va[:, :], E / 4.0, vb[:, :], ALU.mult, ALU.add))
                ts(vb[:, :], va[:, :], 1.0 / E, None, ALU.mult).then_inc(norm_sync, 1)
                dve.wait_ge(norm_sync, 1)
                step(ts(va[:, :], vb[:, :], EPS, None, ALU.add))
                dve.wait_ge(std_ready, 1)
                step(nc.vector.reciprocal(rstd[:, :], vc[:, :]))
                step(tt(vb[:, :], rstd[:, :], rstd[:, :], ALU.mult))
                step(tt(vb[:, :], vb[:, :], va[:, :], ALU.mult))
                step(ts(vb[:, :], vb[:, :], -0.5, 1.5, ALU.mult, ALU.add))
                step(tt(rstd[:, :], rstd[:, :], vb[:, :], ALU.mult))
                norm(0, 0)
                route(0, 0, 0)
                route(0, 0, 1)
                for hp in range(HP):
                    rounds(0, hp)
                    if hp >= 1:
                        absolutes(0, 0, hp - 1)
                absolutes(0, 0, HP - 1)
                rotate(0, 0, 0)
                dve.wait_ge(weights_in, 16 * WEIGHT_LOADS)
                gate(0, 0, range(INNER))

            def steps(b, par, more):
                for k in range(NH + (0 if more else 2)):
                    lb, g, there = lagged(b, k, 2)
                    if there:
                        combine(lb, g, par if k >= 2 else 1 - par)
                    if k < NH and k % 2 == 0:
                        hp = (k + 2) // 2
                        if hp < HP:
                            rotate(b, hp, par)
                        elif more:
                            rotate(b + 1, 0, 1 - par)
                    if k < NH:
                        negate(b, k)
                    if k == 3 and not first(b):
                        finish(b - 1, 1 - par)
                    if not more:
                        continue
                    if k == 0:
                        norm(b + 1, 1 - par)
                    if k == 1:
                        route(b + 1, 1 - par, 0)
                    if k == 4:
                        route(b + 1, 1 - par, 1)
                    if 6 <= k < 10:
                        rounds(b + 1, 2 * (k - 6))
                        rounds(b + 1, 2 * (k - 6) + 1)
                    if 7 <= k < 11:
                        absolutes(b + 1, 1 - par, 2 * (k - 7))
                        absolutes(b + 1, 1 - par, 2 * (k - 7) + 1)
                    if 12 <= k:
                        gate(b + 1, 1 - par, range(4 * (k - 12), 4 * (k - 12) + 4))

            body(dve, steps, prologue)
            finish(B - 1, (B - 1) % 2)

        @block.gpsimd
        def _(pool):
            tt = nc.gpsimd.tensor_tensor

            def part_turns(nb, par, hp):
                pool.wait_ge(whole_made, HP * nb + hp + 1)
                wait(pool, k_prod, HP * (nb - 1))
                tt(cs[:, par, hp, 1, :], turns[:, hp % 2], whole[:, hp % 2], ALU.subtract).then_inc(frac_made, 1)

            def add_rotated(b, hp):
                H, r = b * HP + hp, hp % 2
                wait(pool, qk_in[r], 64 * (b * (HP // 2) + hp // 2))
                for what, prod_done in enumerate((q_prod, k_prod)):
                    pool.wait_ge(prod_done, H + 1)
                    tt(rot[:, r, what], prod[:, what, 0], prod[:, what, 1], ALU.add).then_inc(rot_made, 1)

            def add_slots(b, g):
                G, r = b * NH + g, g % 2
                pool.wait_ge(exp_made, 3 * G + 1)
                wait(pool, probs_made, G - 1)
                e = expd[:, r, 0].rearrange("p (s t j) -> p s t j", s=2, t=2)
                tt(sums[:, r, 0:256].rearrange("p (s j) -> p s j", s=2), e[:, :, 0], e[:, :, 1], ALU.add).then_inc(slots_added, 1)
                pool.wait_ge(exp_made, 3 * G + 3)
                tt(sums[:, r, 256:768].rearrange("p (s j) -> p s j", s=2), expd[:, r, 1:3, 0:256], expd[:, r, 1:3, 256:512],
                   ALU.add).then_inc(slots_added, 1)

            def prologue():
                nc.gpsimd.memset(wout_sb[:, :, :], 0.0).then_inc(zeroed, 1)
                nc.gpsimd.memset(qk[:, :, :, :, :], 0.0).then_inc(zeroed, 1)
                pool.wait_ge(weights_in, 16 * WEIGHT_LOADS)
                halves = lambda t: t.rearrange("p (h c f) -> p h c f", c=2, f=F)
                q_from, q_to = halves(wq_sb[:, :]), halves(wq_rot[:, :])
                nc.gpsimd.tensor_scalar(q_to[:, :, 0], q_from[:, :, 1], -1.0, None, ALU.mult).then_inc(weights_made, 1)
                nc.gpsimd.tensor_copy(q_to[:, :, 1], q_from[:, :, 0]).then_inc(weights_made, 1)
                k_from = halves(wk_in)
                both = lambda v: v.rearrange("p h (o f) -> p h o f", o=1).broadcast_to([128, NKV, 2, v.shape[-1]])
                nc.gpsimd.tensor_copy(wk_two[:, :, :, :], both(wk_in.rearrange("p (h d) -> p h d", h=NKV))).then_inc(weights_made, 1)
                nc.gpsimd.tensor_scalar(wk_rot[:, :, :, 0:F], both(k_from[:, :, 1]), -1.0, None, ALU.mult).then_inc(weights_made, 1)
                nc.gpsimd.tensor_copy(wk_rot[:, :, :, F:D], both(k_from[:, :, 0])).then_inc(weights_made, 1)
                for hp in range(HP):
                    part_turns(0, 0, hp)
                add_rotated(0, 0)

            def steps(b, par, more):
                for k in range(NH + (0 if more else 1)):
                    if k < NH and k % 2 == 0:
                        hp = (k + 2) // 2
                        if hp < HP:
                            add_rotated(b, hp)
                        elif more:
                            add_rotated(b + 1, 0)
                    lb, g, there = lagged(b, k, 1)
                    if there:
                        add_slots(lb, g)
                    if more and 6 <= k < 10:
                        part_turns(b + 1, 1 - par, 2 * (k - 6))
                        part_turns(b + 1, 1 - par, 2 * (k - 6) + 1)

            body(pool, steps, prologue)


_INS = ["L0_attn_x", "L0_attn_wq", "L0_attn_wk", "L0_attn_wv", "L0_attn_wr", "L0_attn_wo", "L0_ffn_Win", "L0_ffn_bin_",
        "L0_ffn_W1", "L0_ffn_b1", "L0_ffn_W2", "L0_ffn_b2", "L0_ffn_Wout", "L0_ffn_bout"]


def kernel(**inputs):
    import numpy as _np
    import concourse.bacc as _bacc
    from concourse import mybir as _mybir
    from concourse.bass_utils import run_bass_kernel_spmd as _run

    nc = _bacc.Bacc("TRN2", target_bir_lowering=False, num_devices=1)
    arrays, args = {}, []
    for name in _INS:
        a = _np.ascontiguousarray(inputs[name])
        arrays[f"in_{name}_dram"] = a
        args.append(nc.dram_tensor(f"in_{name}_dram", a.shape, _mybir.dt.from_np(a.dtype), kind="ExternalInput").ap())
    arrays["shape_constants"] = shape_constants()
    args.append(nc.dram_tensor("shape_constants", (128, C_COLS), _mybir.dt.float32, kind="ExternalInput").ap())
    args.append(nc.dram_tensor("out_0_dram", (B, N, E), _mybir.dt.float32, kind="ExternalOutput").ap())
    routed_attention_block(nc, *args)
    r = _run(nc, [arrays], core_ids=[0])
    return r.results[0]["out_0_dram"]
```

```python
import concourse.bass as bass
from concourse import mybir
from contextlib import ExitStack

import numpy as np

B, N, E = 32, 256, 128
NH, NKV, D, ND = 16, 4, 64, 4
HP = NH // 2
NB = N // 128
F = D // 2
GH = 128 // F
NG = NH // GH
M, INNER = 64, 16
SCALE = float(D) ** -0.5
BIG = 1.0e9
EPS = 1.0e-5
ROUND = 12582912.0
TURN = 6.283185
C_ID, C_TRI, C_BEFORE, C_FREQ, C_COLS = 0, 128, 256, 384, 385


def shape_constants():
    c = np.zeros((128, C_COLS), np.float32)
    row, col = np.arange(128)[:, None], np.arange(128)[None, :]
    c[:, C_ID:C_ID + 128] = row == col
    c[:, C_TRI:C_TRI + 128] = np.where(col > row, -BIG, 0.0)
    c[:, C_BEFORE:C_BEFORE + 128] = row < col
    freq = 1.0 / 10000.0 ** (np.arange(0, D, 2, dtype=np.float64) / D)
    c[:, C_FREQ] = (freq / (2 * np.pi)).astype(np.float32)[np.arange(128) % F]
    return c


def routed_attention_block(nc, x, wq, wk, wv, wr, wo, Win, bin_, W1, b1, W2, b2, Wout, bout, consts, out):
    fp32, bf16 = mybir.dt.float32, mybir.dt.bfloat16
    ALU, ACT, AX = mybir.AluOpType, mybir.ActivationFunctionType, mybir.AxisListType

    ctx = ExitStack()
    with ctx:
        def sb(name, shape, dt=fp32):
            return ctx.enter_context(nc.sbuf_tensor(name, shape, dt))

        def sem(name):
            return ctx.enter_context(nc.semaphore(name))

        cst = sb("cst", [128, C_COLS])
        ident = cst[:, C_ID:C_ID + 128]
        ident_bf = sb("ident_bf", [128, 128], bf16)
        before_bf = sb("before_bf", [128, 128], bf16)
        ones_bf = sb("ones_bf", [128, 128], bf16)
        causal0 = sb("causal0", [128, 2, 128])
        causal1 = sb("causal1", [128, 2, 256])
        quarter = sb("quarter", [128, 1])
        eps = sb("eps", [128, 1])
        wq_sb = sb("wq_sb", [128, NH * D])
        wq_rot = sb("wq_rot", [128, NH * D])
        wk_two = sb("wk_two", [128, NKV, 2, D])
        wk_rot = sb("wk_rot", [128, NKV, 2, D])
        wv_sb = sb("wv_sb", [128, NKV * D])
        wr_sb = sb("wr_sb", [128, NH * ND])
        wo_sb = sb("wo_sb", [128, HP, E])
        win_sb = sb("win_sb", [128, M])
        wout_sb = sb("wout_sb", [128, NB, E])
        bin_sb = sb("bin_sb", [128, 1])
        b2_sb = sb("b2_sb", [128, 1])
        w1_sb = sb("w1_sb", [128, INNER])
        b1_sb = sb("b1_sb", [128, INNER])
        w2_sb = sb("w2_sb", [128, INNER])
        bout_sb = sb("bout_sb", [128, E])
        mean = sb("mean", [128, B * NB])
        rstd = sb("rstd", [128, B * NB])
        va, vb, vc = (sb(n, [128, B * NB]) for n in ("va", "vb", "vc"))
        x_ln = sb("x_ln", [128, 2, NB, E])
        x_res = sb("x_res", [128, 2, NB, E])
        xn = sb("xn", [128, NB, E])
        xnT = sb("xnT", [128, 2, N])
        lg = sb("lg", [128, NB * NH, ND])
        ge0 = sb("ge0", [128, NB * NH, 3])
        ge1 = sb("ge1", [128, NB * NH, 2])
        ge2 = sb("ge2", [128, NB * NH, 1])
        win = sb("win", [128, NB * NH, ND])
        mem = sb("mem", [128, NB * NH, ND])
        mem_bf = sb("mem_bf", [128, NB * NH, ND], bf16)
        low = sb("low", [128, NB * NH, 1])
        slot = sb("slot", [128, 2, NB * NH, ND])
        sel = sb("sel", [128, NB * NH, 2, ND])
        sv = sb("sv", [128, NB * NH, 2])
        se = sb("se", [128, NB * NH, 2])
        smax = sb("smax", [128, NB * NH, 1])
        ssum = sb("ssum", [128, NB * NH, 1])
        wslot = sb("wslot", [128, 2, NB, NH, 2])
        pos_bf = sb("pos_bf", [128, NB * NH, 2], bf16)
        code = sb("code", [64, 2, 2, 2 * N])
        turns = sb("turns", [128, 2, 2 * N])
        whole = sb("whole", [128, 2, 2 * N])
        cs = sb("cs", [128, 2, NG, 2, 2 * N])
        pair_cs = sb("pair_cs", [128, 2, 2, 2 * N])
        prod = sb("prod", [128, 2, 2, 2 * N])
        rot = sb("rot", [128, 2, 2, 2 * N])
        qk = sb("qk", [128, 2, 2, 2, 2 * N])
        neg_s = sb("neg_s", [128, 2, 3, 512])
        neg_max = sb("neg_max", [128, 2, 4])
        expd = sb("expd", [128, 2, 3, 512])
        total = sb("total", [128, 2, 4])
        recip = sb("recip", [128, 2, 4])
        coef = sb("coef", [128, 2, 4])
        sums = sb("sums", [128, 2, 768])
        probs = sb("probs", [128, 2, 384])
        probsT = sb("probsT", [128, 2, 384])
        v_sb = sb("v_sb", [128, 2, NB, NKV * D])
        yT = sb("yT", [128, 2, HP, N])
        sT = sb("sT", [128, 2, 128])
        hT = sb("hT", [128, 4, 128])
        gT = sb("gT", [128, 2, 128])
        part = sb("part", [128, NB, E])
        res = sb("res", [128, 2, NB, E])

        wk_in = prod[:, 0, 0, 0:NKV * D]
        st = expd[:, 0, 0, 0:B * NB * 6].rearrange("p (t c) -> p t c", c=6)

        def pb(name):
            return ctx.enter_context(nc.psum_tensor(name, [128, 512], fp32))

        p_score = [pb(f"p_score{u}") for u in range(3)]
        p_q, p_k, p_misc, p_pt, p_y = (pb(n) for n in ("p_q", "p_k", "p_misc", "p_pt", "p_y"))

        consts_in, weights_in = sem("consts_in"), sem("weights_in")
        x_all_in, norm_step, std_ready = sem("x_all_in"), sem("norm_step"), sem("std_ready")
        norm_sync, weights_made, consts_made = sem("norm_sync"), sem("weights_made"), sem("consts_made")
        zeroed, stats_read = sem("zeroed"), sem("stats_read")
        x_ln_in = [sem("x_ln_in0"), sem("x_ln_in1")]
        x_res_in = [sem("x_res_in0"), sem("x_res_in1")]
        stored = [sem("stored0"), sem("stored1")]
        xn_made, xnT_mm, xnT_made = sem("xn_made"), sem("xnT_mm"), sem("xnT_made")
        logits_mm, logits_made, sT_made = sem("logits_mm"), sem("logits_made"), sem("sT_made")
        route_step, mem_made, slot_made, slot_exp = sem("route_step"), sem("mem_made"), sem("slot_made"), sem("slot_exp")
        diff_made, wslot_made = sem("diff_made"), sem("wslot_made")
        pos_mm, pos_sel, pos_made = sem("pos_mm"), sem("pos_sel"), sem("pos_made")
        code_mm, code_made = sem("code_mm"), sem("code_made")
        v_mm, v_made = sem("v_mm"), sem("v_made")
        turn_mm, turn_made, whole_made = sem("turn_mm"), sem("turn_made"), sem("whole_made")
        frac_made, abs_made, table_made = sem("frac_made"), sem("abs_made"), sem("table_made")
        q_mm, k_mm, q_prod, k_prod = sem("q_mm"), sem("k_mm"), sem("q_prod"), sem("k_prod")
        rot_made = sem("rot_made")
        qk_in = [sem("qk_in0"), sem("qk_in1")]
        first_table_made = sem("first_table_made")
        pair_cs_in = [sem("pair_cs_in0"), sem("pair_cs_in1")]
        score_mm, score_neg, exp_made, slots_added = sem("score_mm"), sem("score_neg"), sem("exp_made"), sem("slots_added")
        coef_step, probs_made, pt_mm, pt_made = sem("coef_step"), sem("probs_made"), sem("pt_mm"), sem("pt_made")
        y_mm, yT_made = sem("y_mm"), sem("yT_made")
        relu_made, g_step = sem("relu_made"), sem("g_step")
        pe_waited, dve_waited = sem("pe_waited"), sem("dve_waited")
        out_mm, out_read, out_made = sem("out_mm"), sem("out_read"), sem("out_made")

        WEIGHT_LOADS = 7 + 6 * NB

        x_tok = x.rearrange("b (n p) e -> p b n e", p=128)
        out_tok = out.rearrange("b (n p) e -> p b n e", p=128)

        def wait(eng, s, value):
            if not (isinstance(value, int) and value <= 0):
                eng.wait_ge(s, value)

        def first(b):
            return isinstance(b, int) and b == 0

        def loads_of(b, par):
            return b * 8 + (16 - 8 * par)

        def body(eng, steps, prologue):
            prologue()
            steps(0, 0, True)
            with eng.Fori(0, (B - 2) // 2) as i:
                steps(i * 2 + 1, 1, True)
                steps(i * 2 + 2, 0, True)
            steps(B - 1, 1, False)

        def lagged(b, k, lag):
            g = k - lag
            if g < 0:
                return b - 1, g + NH, not first(b)
            return b, g, g < NH

        def rotated(b, k, more):
            parts = {NH - 4: [], NH - 3: [(HP, 0), (HP, 1)]}.get(k, [(k // 2 + 2, k % 2)])
            here = [(b, hp, what) for hp, what in parts if hp < HP]
            return here + [(b + 1, hp - HP, what) for hp, what in parts if hp >= HP and more]

        block = ctx.enter_context(nc.Block())

        @block.sync
        def _(sp):
            def load_ln(nb, par):
                wait(sp, xn_made, nb - 1)
                sp.dma_start(x_ln[:, par], x_tok[:, bass.ds(nb, 1)]).then_inc(x_ln_in[par], 16)

            def place(b, hp, par):
                H, r = b * HP + hp, hp % 2
                wait(sp, score_mm, 6 * H - 6)
                if hp == 0:
                    sp.wait_ge(code_made, 2 * b + 2)
                for h in range(2):
                    head = 2 * hp + h
                    c0 = 64 - 64 * h
                    sp.dma_start(qk[c0:c0 + ND, r, :, h, :], code[ND * head:ND * head + ND, par]).then_inc(qk_in[r], 16)
                wait(sp, rot_made, 2 * H + 2)
                for h in range(2):
                    sp.dma_start(qk[64 * h:64 * h + 64, r, :, h, :], rot[64 * h:64 * h + 64, r]).then_inc(qk_in[r], 16)

            def replicate(b, hp, par):
                H, r = b * HP + hp, hp % 2
                wait(sp, k_prod, H - 1)
                if hp == 0:
                    sp.wait_ge(first_table_made, 2 * b + 2)
                if hp == GH // 2:
                    sp.wait_ge(table_made, 2 * b + 2)
                for h in range(2):
                    rows = cs[64 * (hp % 2) + F * h:64 * (hp % 2) + F * h + F, par, hp // 2]
                    for half in range(2):
                        to = 64 * h + F * half
                        sp.dma_start(pair_cs[to:to + F, r], rows).then_inc(pair_cs_in[r], 16)

            def prologue():
                sp.dma_start(cst[:, :], consts).then_inc(consts_in, 16)
                stage = cs[:, :, :, :, :].rearrange("p q a b c -> p (q a b c)").rearrange("p (t n e) -> p t n e", t=B, n=NB)
                for q in range(4):
                    sp.dma_start(stage[:, 8 * q:8 * q + 8], x_tok[:, 8 * q:8 * q + 8]).then_inc(x_all_in, 16)
                sp.dma_start(wq_sb[:, :], wq).then_inc(weights_in, 16)
                sp.dma_start(wk_in, wk).then_inc(weights_in, 16)
                sp.dma_start(wv_sb[:, :], wv).then_inc(weights_in, 16)
                sp.dma_start(wr_sb[:, :], wr).then_inc(weights_in, 16)
                sp.dma_start(wo_sb[:, :, :], wo.rearrange("(h p) e -> p h e", p=128)).then_inc(weights_in, 16)
                sp.dma_start(win_sb[:, :], Win).then_inc(weights_in, 16)
                sp.dma_start(bout_sb[:, :], bout.rearrange("(o e) -> o e", o=1).broadcast_to([128, E])).then_inc(weights_in, 16)
                col = lambda v: v.rearrange("(m o) -> m o", o=1)
                for blk in range(NB):
                    rows = slice(64 * blk, 64 * blk + 64)
                    for dst, src in ((w1_sb, W1), (b1_sb, b1), (w2_sb, W2)):
                        sp.dma_start(dst[rows, :], src).then_inc(weights_in, 16)
                    sp.dma_start(bin_sb[rows, :], col(bin_)).then_inc(weights_in, 16)
                    sp.dma_start(b2_sb[rows, :], col(b2)).then_inc(weights_in, 16)
                load_ln(0, 0)
                sp.dma_start(x_res[:, 0], x_tok[:, 0:1]).then_inc(x_res_in[0], 16)
                sp.wait_ge(zeroed, 2)
                for blk in range(NB):
                    sp.dma_start(wout_sb[64 * blk:64 * blk + 64, blk, :], Wout).then_inc(weights_in, 16)
                replicate(0, 0, 0)
                replicate(0, 1, 0)
                place(0, 0, 0)
                replicate(0, 2, 0)
                place(0, 1, 0)

            def steps(b, par, more):
                for k in range(NH):
                    if k == 0 and more:
                        load_ln(b + 1, 1 - par)
                    if k == NH - 1:
                        if not first(b):
                            sp.wait_ge(out_made, b)
                            sp.dma_start(out_tok[:, bass.ds(b - 1, 1)], res[:, 1 - par]).then_inc(stored[1 - par], 16)
                        if more:
                            if not first(b):
                                sp.wait_ge(stored[1 - par], loads_of(b - 1, 1 - par))
                            sp.dma_start(x_res[:, 1 - par], x_tok[:, bass.ds(b + 1, 1)]).then_inc(x_res_in[1 - par], 16)
                    if k % 2 == 1:
                        ahead = (k + 5) // 2
                        if ahead < HP:
                            replicate(b, ahead, par)
                        elif more and ahead > HP:
                            replicate(b + 1, ahead - HP, 1 - par)
                        now = (k + 3) // 2
                        if now < HP:
                            place(b, now, par)
                        elif more:
                            place(b + 1, now - HP, 1 - par)
                    if k == NH - 4 and more:
                        replicate(b + 1, 0, 1 - par)

            body(sp, steps, prologue)
            sp.wait_ge(out_made, B)
            sp.dma_start(out_tok[:, B - 1:B], res[:, (B - 1) % 2]).then_inc(stored[(B - 1) % 2], 16)
            sp.wait_ge(stored[0], 16 * (B // 2))
            sp.wait_ge(stored[1], 16 * (B // 2))

        @block.tensor
        def _(pe):
            mm = nc.tensor.matmul

            def transpose_x(nb, par):
                pe.wait_ge(xn_made, nb + 1)
                wait(pe, out_read, nb - 2)
                for blk in range(NB):
                    last = nc.tensor.transpose(p_misc[:, 128 * blk:128 * blk + 128], xn[:, blk, :], ident)
                last.then_inc(xnT_mm, 1)

            def logits(nb, par):
                pe.wait_ge(xnT_made, nb + 1)
                for blk in range(NB):
                    mm(p_misc[:, 64 * blk:64 * blk + 64], xnT[:, par, 128 * blk:128 * blk + 128], wr_sb[:, :],
                       start=True, stop=True)
                for blk in range(NB):
                    last = mm(p_misc[64 * blk:64 * blk + 64, 128:256], win_sb[:, :],
                              xnT[:, par, 128 * blk:128 * blk + 128], start=True, stop=True)
                last.then_inc(logits_mm, 1)

            def values(nb, par):
                pe.wait_ge(logits_made, nb + 1)
                pe.wait_ge(sT_made, nb + 1)
                for blk in range(NB):
                    last = mm(p_misc[:, 256 * blk:256 * blk + 256], xnT[:, par, 128 * blk:128 * blk + 128],
                              wv_sb[:, :], start=True, stop=True)
                last.then_inc(v_mm, 1)

            def positions(nb, par):
                pe.wait_ge(mem_made, nb + 1)
                pe.wait_ge(v_made, nb + 1)
                m = mem_bf[:, :, :].rearrange("p (n h) d -> p n (h d)", n=NB)
                mm(p_misc[:, 0:64], before_bf[:, :], m[:, 0], start=True, stop=True)
                mm(p_misc[:, 64:128], ones_bf[:, :], m[:, 0], start=True, stop=False)
                mm(p_misc[:, 64:128], before_bf[:, :], m[:, 1], start=False, stop=True).then_inc(pos_mm, 1)

            def codes(nb, par):
                pe.wait_ge(slot_made, nb + 1)
                pe.wait_ge(pos_sel, nb + 1)
                pe.sem_inc(pe_waited, 1)
                for s in range(2):
                    for blk in range(NB):
                        at = 256 * s + 128 * blk
                        last = nc.tensor.transpose(p_misc[0:64, at:at + 128], slot[:, s, NH * blk:NH * blk + NH, :].rearrange("p h d -> p (h d)"), ident)
                last.then_inc(code_mm, 1)

            def turn(nb, t):
                if t == 0:
                    pe.wait_ge(pos_made, nb + 1)
                    pe.wait_ge(code_made, 2 * nb + 2)
                wait(pe, turn_made, NG * nb + t)
                for s in range(2):
                    for blk in range(NB):
                        at = 256 * s + 128 * blk
                        for h in range(GH):
                            one = pos_bf[:, NH * blk + GH * t + h, s:s + 1].broadcast_to([128, F])
                            last = mm(p_misc[F * h:F * h + F, at:at + 128], one, ident_bf[:, :], start=True, stop=True)
                last.then_inc(turn_mm, 1)

            def project_q(b, hp, par):
                pe.wait_ge(xnT_made, b + 1)
                wait(pe, q_prod, b * HP + hp)
                mm(p_q[:, 0:256], wq_sb[:, 128 * hp:128 * hp + 128], xnT[:, par], start=True, stop=True)
                mm(p_q[:, 256:512], wq_rot[:, 128 * hp:128 * hp + 128], xnT[:, par], start=True, stop=True).then_inc(q_mm, 1)

            def project_k(b, hp, par):
                wait(pe, k_prod, b * HP + hp)
                kv = hp // 2
                mm(p_k[:, 0:256], wk_two[:, kv].rearrange("p a d -> p (a d)"), xnT[:, par], start=True, stop=True)
                mm(p_k[:, 256:512], wk_rot[:, kv].rearrange("p a d -> p (a d)"), xnT[:, par],
                   start=True, stop=True).then_inc(k_mm, 1)

            def scores(b, g):
                G, h, r = b * NH + g, g % 2, (g // 2) % 2
                H_in_ring = b * (HP // 2) + g // 4
                if h == 0:
                    pe.wait_ge(qk_in[r], 64 * H_in_ring + 64)
                q, key = qk[:, r, 0, h, :], qk[:, r, 1, h, :].rearrange("p (t j) -> p t j", t=2)
                wait(pe, score_neg, 3 * G - 2)
                for s in range(2):
                    last = mm(p_score[0][:, 256 * s:256 * s + 256], q[:, 256 * s:256 * s + 128], key[:, :, 0:128],
                              start=True, stop=True)
                last.then_inc(score_mm, 1)
                for s in range(2):
                    wait(pe, score_neg, 3 * G - 1 + s)
                    mm(p_score[1 + s][:, :], q[:, 256 * s + 128:256 * s + 256], key, start=True, stop=True).then_inc(score_mm, 1)

            def transpose_probs(b, g):
                G = b * NH + g
                pe.wait_ge(probs_made, G + 1)
                wait(pe, pt_made, G)
                for j in range(3):
                    last = nc.tensor.transpose(p_pt[:, 128 * j:128 * j + 128], probs[:, g % 2, 128 * j:128 * j + 128], ident)
                last.then_inc(pt_mm, 1)

            def mix_values(b, g, par):
                G, h, kv = b * NH + g, g % 2, g // (NH // NKV)
                pe.wait_ge(pt_made, G + 1)
                pe.wait_ge(v_made, b + 1)
                if h == 0:
                    wait(pe, yT_made, b * HP + g // 2)
                rows, vs = slice(64 * h, 64 * h + 64), slice(D * kv, D * kv + D)
                mm(p_y[rows, 0:256], v_sb[:, par, 0, vs], probsT[:, g % 2, 0:256], start=True, stop=False)
                mm(p_y[rows, 128:256], v_sb[:, par, 1, vs], probsT[:, g % 2, 256:384], start=False, stop=True).then_inc(y_mm, 1)

            def project_out(b, par, blk):
                pe.wait_ge(yT_made, HP * b + HP)
                pe.wait_ge(g_step, INNER * (b + 1))
                o = p_misc[:, 128 * blk:128 * blk + 128]
                for hp in range(HP):
                    mm(o, yT[:, par, hp, 128 * blk:128 * blk + 128], wo_sb[:, hp, :], start=(hp == 0), stop=False)
                mm(o, gT[:, par, :], wout_sb[:, blk, :], start=False, stop=True).then_inc(out_mm, 1)

            def prologue():
                pe.wait_ge(consts_in, 16)
                pe.wait_ge(consts_made, 3)
                pe.wait_ge(weights_in, 16 * WEIGHT_LOADS)
                pe.wait_ge(weights_made, 5)
                transpose_x(0, 0)
                logits(0, 0)
                values(0, 0)
                positions(0, 0)
                codes(0, 0)
                for t in range(NG):
                    turn(0, t)
                project_q(0, 0, 0)
                project_k(0, 0, 0)
                project_q(0, 1, 0)
                project_q(0, 2, 0)

            def steps(b, par, more):
                for k in range(NH + (0 if more else 4)):
                    if k < NH:
                        scores(b, k)
                    lb, g, there = lagged(b, k, 3)
                    if there:
                        transpose_probs(lb, g)
                    lb, g, there = lagged(b, k, 4)
                    if there:
                        mix_values(lb, g, par if k >= 4 else 1 - par)
                    if k < NH and k % 2 == 1:
                        hp = (k + 5) // 2
                        if hp < HP:
                            project_q(b, hp, par)
                        elif more and hp != HP + 1:
                            project_q(b + 1, hp - HP, 1 - par)
                    if more and k == NH - 2:
                        project_q(b + 1, 1, 1 - par)
                    if k < NH and k % 4 == 0:
                        hp = k // 2 + 2
                        if hp < HP:
                            project_k(b, hp, par)
                        elif more:
                            project_k(b + 1, 0, 1 - par)
                    if more and k == 0:
                        transpose_x(b + 1, 1 - par)
                    if more and k == 1:
                        logits(b + 1, 1 - par)
                    if more and k == 2:
                        values(b + 1, 1 - par)
                    if more and k == 3:
                        positions(b + 1, 1 - par)
                    if more and k == 5:
                        codes(b + 1, 1 - par)
                    if more and 6 <= k < 6 + NG:
                        turn(b + 1, k - 6)
                    if k == 11 and not first(b):
                        if more:
                            pe.wait_ge(turn_made, NG * (b + 2))
                        else:
                            pe.wait_ge(out_read, b - 1)
                        project_out(b - 1, 1 - par, 0)
                    if k == 12 and not first(b):
                        project_out(b - 1, 1 - par, 1)

            body(pe, steps, prologue)
            pe.wait_ge(out_read, B - 1)
            for blk in range(NB):
                project_out(B - 1, (B - 1) % 2, blk)

        @block.scalar
        def _(act):
            fn = nc.scalar.activation

            def keep_xT(nb, par):
                act.wait_ge(xnT_mm, nb + 1)
                wait(act, q_mm, HP * (nb - 1))
                fn(xnT[:, par], p_misc[:, 0:256], ACT.Copy).then_inc(xnT_made, 1)

            def keep_logits(nb, par):
                act.wait_ge(logits_mm, nb + 1)
                wait(act, wslot_made, nb)
                wait(act, relu_made, INNER * (nb - 1))
                fn(lg[:, :, :].rearrange("p a d -> p (a d)"), p_misc[:, 0:128], ACT.Copy).then_inc(logits_made, 1)
                fn(sT[:, par], p_misc[:, 128:256], ACT.Identity, bias=bin_sb[:, 0:1]).then_inc(sT_made, 1)

            def keep_values(nb, par):
                act.wait_ge(v_mm, nb + 1)
                wait(act, y_mm, NH * (nb - 1))
                fn(v_sb[:, par].rearrange("p n d -> p (n d)"), p_misc[:, :], ACT.Copy).then_inc(v_made, 1)

            def slot_exps(nb):
                act.wait_ge(diff_made, nb + 1)
                wait(act, wslot_made, nb)
                fn(se[:, :, :], sv[:, :, :], ACT.Exp).then_inc(slot_exp, 1)

            def keep_codes(nb, par):
                act.wait_ge(code_mm, nb + 1)
                for r in range(2):
                    wait(act, qk_in[r], 64 * (HP // 2) * (nb - 1))
                fn(code[:, par, 0, :], p_misc[0:64, :], ACT.Copy, scale=-1.0, bias=1.0).then_inc(code_made, 1)
                fn(code[:, par, 1, :], p_misc[0:64, :], ACT.Copy, scale=-BIG).then_inc(code_made, 1)

            def keep_turns(nb, t):
                act.wait_ge(turn_mm, NG * nb + t + 1)
                wait(act, frac_made, NG * nb + t - 1)
                fn(turns[:, t % 2], p_misc[:, :], ACT.Copy, scale=cst[:, C_FREQ:C_FREQ + 1]).then_inc(turn_made, 1)

            def trig(nb, par):
                act.wait_ge(abs_made, NG * (nb + 1))
                for groups, done in ((slice(0, 1), first_table_made), (slice(1, NG), table_made)):
                    cos, sin = cs[:, par, groups, 0, :], cs[:, par, groups, 1, :]
                    fn(cos, cos, ACT.Sin, bias=quarter[:, 0:1], scale=-TURN).then_inc(done, 1)
                    fn(sin, sin, ACT.Sin, scale=TURN).then_inc(done, 1)

            def relus(b, par, js):
                for j in js:
                    act.wait_ge(sT_made, b + 1)
                    wait(act, g_step, INNER * b + j - 3)
                    fn(hT[:, j % 4], sT[:, par], ACT.Relu, bias=b1_sb[:, j:j + 1], scale=w1_sb[:, j:j + 1]).then_inc(relu_made, 1)

            def exps(b, g):
                G, r = b * NH + g, g % 2
                act.wait_ge(score_neg, 3 * G + 1)
                wait(act, slots_added, 2 * G - 3)
                wait(act, probs_made, G - 1)
                for s in range(2):
                    last = fn(expd[:, r, 0, 256 * s:256 * s + 256], neg_s[:, r, 0, 256 * s:256 * s + 256], ACT.Exp,
                              bias=neg_max[:, r, s:s + 1], scale=-1.0, accum_out=total[:, r, s:s + 1])
                last.then_inc(exp_made, 1)
                wait(act, slots_added, 2 * G - 2)
                for s in range(2):
                    act.wait_ge(score_neg, 3 * G + 2 + s)
                    fn(expd[:, r, 1 + s, :], neg_s[:, r, 1 + s, :], ACT.Exp, bias=neg_max[:, r, 2 + s:3 + s], scale=-1.0,
                       accum_out=total[:, r, 2 + s:3 + s]).then_inc(exp_made, 1)

            def keep_probsT(b, g):
                G = b * NH + g
                act.wait_ge(pt_mm, G + 1)
                wait(act, y_mm, G - 1)
                fn(probsT[:, g % 2], p_pt[:, 0:384], ACT.Copy).then_inc(pt_made, 1)

            def keep_yT(b, hp, par):
                act.wait_ge(y_mm, 2 * (b * HP + hp) + 2)
                if hp == 0:
                    wait(act, out_mm, NB * (b - 1))
                fn(yT[:, par, hp], p_y[:, 0:256], ACT.Copy).then_inc(yT_made, 1)

            def prologue():
                act.wait_ge(norm_sync, 1)
                fn(vc[:, :], vb[:, :], ACT.Sqrt, bias=eps[:, 0:1]).then_inc(std_ready, 1)
                keep_xT(0, 0)
                keep_logits(0, 0)
                keep_values(0, 0)
                slot_exps(0)
                keep_codes(0, 0)
                for t in range(NG):
                    keep_turns(0, t)
                trig(0, 0)

            def steps(b, par, more):
                for k in range(NH + (0 if more else 4)):
                    if more and k == 5:
                        slot_exps(b + 1)
                    if more and k == 12:
                        trig(b + 1, 1 - par)
                    lb, g, there = lagged(b, k, 1)
                    if there:
                        exps(lb, g)
                    lb, g, there = lagged(b, k, 3)
                    if there:
                        keep_probsT(lb, g)
                    lb, g, there = lagged(b, k, 4)
                    if there and g % 2 == 1:
                        keep_yT(lb, g // 2, par if k >= 4 else 1 - par)
                    if 2 <= k < 2 + INNER // 2:
                        relus(b, par, range(2 * (k - 2), 2 * (k - 2) + 2))
                    if not more:
                        continue
                    if k == 0:
                        keep_xT(b + 1, 1 - par)
                    if k == 1:
                        keep_logits(b + 1, 1 - par)
                    if k == 2:
                        keep_values(b + 1, 1 - par)
                    if k == 5:
                        keep_codes(b + 1, 1 - par)
                    if 6 <= k < 6 + NG:
                        keep_turns(b + 1, k - 6)

            body(act, steps, prologue)

        @block.vector
        def _(dve):
            tt, ts, stt = nc.vector.tensor_tensor, nc.vector.tensor_scalar, nc.vector.scalar_tensor_tensor
            lgv = lg[:, :, :]

            def norm(nb, par):
                dve.wait_ge(x_ln_in[par], loads_of(nb, par))
                wait(dve, xnT_mm, nb)
                for blk in range(NB):
                    t = nb * NB + blk
                    last = ts(xn[:, blk, :], x_ln[:, par, blk, :], mean[:, bass.ds(t, 1)], rstd[:, bass.ds(t, 1)],
                              ALU.subtract, ALU.mult)
                last.then_inc(xn_made, 1)

            def route(nb, par, stage):
                if stage == 0:
                    dve.wait_ge(logits_made, nb + 1)
                    wait(dve, pos_mm, nb)
                    wait(dve, code_mm, nb)
                elif stage == 11:
                    dve.wait_ge(slot_exp, nb + 1)
                elif stage == 14:
                    dve.wait_ge(pos_mm, nb + 1)
                elif stage == 15:
                    dve.wait_ge(pos_sel, nb + 1)
                else:
                    dve.wait_ge(route_step, 12 * nb + (stage if stage <= 10 else stage - 1))
                l = lambda a, b_: lgv[:, :, a:b_]
                if stage == 0:
                    tt(ge0[:, :, :], l(0, 1).broadcast_to([128, NB * NH, 3]), l(1, 4), ALU.is_ge)
                    tt(ge1[:, :, :], l(1, 2).broadcast_to([128, NB * NH, 2]), l(2, 4), ALU.is_ge)
                    tt(ge2[:, :, :], l(2, 3), l(3, 4), ALU.is_ge).then_inc(route_step, 1)
                elif stage == 1:
                    tt(win[:, :, 0:1], ge0[:, :, 0:1], ge0[:, :, 1:2], ALU.add)
                    tt(win[:, :, 1:2], ge1[:, :, 0:1], ge1[:, :, 1:2], ALU.add)
                    tt(win[:, :, 2:4], ge0[:, :, 1:3], ge1[:, :, :], ALU.add).then_inc(route_step, 1)
                elif stage == 2:
                    tt(win[:, :, 0:1], win[:, :, 0:1], ge0[:, :, 2:3], ALU.add)
                    tt(win[:, :, 1:2], win[:, :, 1:2], ge0[:, :, 0:1], ALU.subtract)
                    tt(win[:, :, 2:3], win[:, :, 2:3], ge2[:, :, :], ALU.subtract)
                    tt(win[:, :, 3:4], win[:, :, 3:4], ge2[:, :, :], ALU.add).then_inc(route_step, 1)
                elif stage == 3:
                    for n, (op, bound) in enumerate(((ALU.is_ge, 2.0), (ALU.is_ge, 1.0), (ALU.is_le, 0.0), (ALU.is_le, 1.0))):
                        last = ts(mem[:, :, n:n + 1], win[:, :, n:n + 1], bound, None, op)
                    last.then_inc(route_step, 1)
                elif stage == 4:
                    nc.vector.tensor_copy(mem_bf[:, :, :], mem[:, :, :]).then_inc(mem_made, 1)
                    nc.vector.tensor_copy(slot[:, 0, :, 0:1], mem[:, :, 0:1])
                    tt(slot[:, 0, :, 1:2], mem[:, :, 1:2], mem[:, :, 0:1], ALU.is_gt)
                    tt(low[:, :, :], mem[:, :, 0:1], mem[:, :, 1:2], ALU.add).then_inc(route_step, 1)
                elif stage == 5:
                    tt(slot[:, 0, :, 2:3], mem[:, :, 2:3], low[:, :, :], ALU.is_gt).then_inc(route_step, 1)
                elif stage == 6:
                    tt(slot[:, 1], mem[:, :, :], slot[:, 0], ALU.subtract).then_inc(route_step, 1)
                elif stage == 7:
                    tt(sel[:, :, 0, :], slot[:, 0], lgv, ALU.mult).then_inc(slot_made, 1)
                    tt(sel[:, :, 1, :], slot[:, 1], lgv, ALU.mult).then_inc(route_step, 1)
                elif stage == 8:
                    nc.vector.tensor_reduce(sv[:, :, :], sel[:, :, :, :], AX.X, ALU.add).then_inc(route_step, 1)
                elif stage == 9:
                    tt(smax[:, :, :], sv[:, :, 0:1], sv[:, :, 1:2], ALU.max).then_inc(route_step, 1)
                elif stage == 10:
                    tt(sv[:, :, :], sv[:, :, :], smax[:, :, :].broadcast_to([128, NB * NH, 2]), ALU.subtract).then_inc(diff_made, 1)
                elif stage == 11:
                    tt(ssum[:, :, :], se[:, :, 0:1], se[:, :, 1:2], ALU.add).then_inc(route_step, 1)
                elif stage == 12:
                    nc.vector.reciprocal(ssum[:, :, :], ssum[:, :, :]).then_inc(route_step, 1)
                elif stage == 13:
                    w = wslot[:, par].rearrange("p n h s -> p (n h) s")
                    tt(w, se[:, :, :], ssum[:, :, :].broadcast_to([128, NB * NH, 2]), ALU.mult).then_inc(wslot_made, 1)
                elif stage == 14:
                    pos = p_misc[:, 0:128].rearrange("p (a d) -> p a d", d=ND)
                    tt(sel[:, :, 0, :], pos, slot[:, 0], ALU.mult)
                    tt(sel[:, :, 1, :], pos, slot[:, 1], ALU.mult).then_inc(pos_sel, 1)
                elif stage == 15:
                    with nc.allow_low_precision(reason="positions are integers below 256, exact in bf16"):
                        nc.vector.tensor_reduce(pos_bf[:, :, :], sel[:, :, :, :], AX.X, ALU.add).then_inc(pos_made, 1)

            def rounds(nb, t):
                dve.wait_ge(turn_made, NG * nb + t + 1)
                wait(dve, frac_made, NG * nb + t - 1)
                ts(whole[:, t % 2], turns[:, t % 2], ROUND, -ROUND, ALU.add, ALU.add).then_inc(whole_made, 1)

            def absolutes(nb, par, t):
                dve.wait_ge(frac_made, NG * nb + t + 1)
                stt(cs[:, par, t, 0, :], cs[:, par, t, 1, :], -1.0, cs[:, par, t, 1, :], ALU.mult, ALU.max).then_inc(abs_made, 1)

            def rotate(b, hp, what):
                H = b * HP + hp
                dve.wait_ge(pair_cs_in[hp % 2], 64 * (b * (HP // 2) + hp // 2 + 1))
                table = pair_cs[:, hp % 2].rearrange("p c (s i) -> p c s i", s=2)
                if what == 0:
                    dve.wait_ge(q_mm, H + 1)
                else:
                    dve.wait_ge(k_mm, b * (HP // 2) + hp // 2 + 1)
                wait(dve, rot_made, 2 * H - 1 + what)
                bank, prod_done = ((p_q, q_prod), (p_k, k_prod))[what]
                for c in range(2):
                    last = tt(prod[:, what, c].rearrange("p (s i) -> p s i", s=2),
                              bank[:, 256 * c:256 * c + 256].rearrange("p (o i) -> p o i", o=1).broadcast_to([128, 2, N]),
                              table[:, c], ALU.mult)
                last.then_inc(prod_done, 1)

            def negate(b, g, unit):
                G, r = b * NH + g, g % 2
                ttr = nc.vector.tensor_tensor_reduce
                dve.wait_ge(score_mm, 3 * G + 1 + unit)
                wait(dve, exp_made, 3 * G - 5 + unit)
                dve.sem_inc(dve_waited, 1)
                if unit == 0:
                    for s in range(2):
                        cols = slice(256 * s, 256 * s + 256)
                        last = ttr(out=neg_s[:, r, 0, cols], in0=p_score[0][:, cols], in1=causal0[:, :, :].rearrange("p t j -> p (t j)"),
                                   scale=-SCALE, scalar=3.0e38, op0=ALU.add, op1=ALU.min, accum_out=neg_max[:, r, s:s + 1])
                else:
                    last = ttr(out=neg_s[:, r, unit, :], in0=p_score[unit][:, :], in1=causal1[:, :, :].rearrange("p t j -> p (t j)"),
                               scale=-SCALE, scalar=3.0e38, op0=ALU.add, op1=ALU.min,
                               accum_out=neg_max[:, r, 1 + unit:2 + unit])
                last.then_inc(score_neg, 1)

            def invert(b, g):
                dve.wait_ge(exp_made, 3 * (b * NH + g) + 3)
                nc.vector.reciprocal(recip[:, g % 2], total[:, g % 2]).then_inc(coef_step, 1)

            def weigh(b, g, par):
                dve.wait_ge(coef_step, 4 * (b * NH + g) + 1)
                tt(coef[:, g % 2].rearrange("p (n s) -> p n s", n=NB), wslot[:, par, :, g, :],
                   recip[:, g % 2].rearrange("p (n s) -> p n s", n=NB), ALU.mult).then_inc(coef_step, 1)

            def combine_low(b, g):
                G, r = b * NH + g, g % 2
                dve.wait_ge(coef_step, 4 * G + 2)
                dve.wait_ge(slots_added, 2 * G + 2)
                wait(dve, pt_mm, G - 1)
                ts(probs[:, r, 0:128], sums[:, r, 0:128], coef[:, r, 0:1], None, ALU.mult).then_inc(coef_step, 1)
                ts(probs[:, r, 128:384], sums[:, r, 256:512], coef[:, r, 2:3], None, ALU.mult).then_inc(coef_step, 1)

            def combine_high(b, g):
                G, r = b * NH + g, g % 2
                p0, p1 = probs[:, r, 0:128], probs[:, r, 128:384]
                dve.wait_ge(coef_step, 4 * G + 4)
                stt(p0, sums[:, r, 128:256], coef[:, r, 1:2], p0, ALU.mult, ALU.add)
                stt(p1, sums[:, r, 512:768], coef[:, r, 3:4], p1, ALU.mult, ALU.add).then_inc(probs_made, 1)

            def gate(b, par, j):
                dve.wait_ge(relu_made, INNER * b + j + 1)
                if j == 0:
                    wait(dve, out_mm, NB * (b - 1))
                    ts(gT[:, par], hT[:, 0], w2_sb[:, 0:1], b2_sb[:, 0:1], ALU.mult, ALU.add).then_inc(g_step, 1)
                else:
                    dve.wait_ge(g_step, INNER * b + j)
                    stt(gT[:, par], hT[:, j % 4], w2_sb[:, j:j + 1], gT[:, par], ALU.mult, ALU.add).then_inc(g_step, 1)

            def add_residual(b, par):
                dve.wait_ge(out_mm, NB * (b + 1))
                dve.wait_ge(x_res_in[par], loads_of(b, par))
                tt(part[:, :, :], p_misc[:, 0:256].rearrange("p (n e) -> p n e", n=NB), x_res[:, par], ALU.add).then_inc(out_read, 1)

            def add_bias(b, par):
                dve.wait_ge(out_read, b + 1)
                for blk in range(NB):
                    last = tt(res[:, par, blk, :], part[:, blk, :], bout_sb[:, :], ALU.add)
                last.then_inc(out_made, 1)

            def prologue():
                dve.wait_ge(consts_in, 16)
                for dst, src in ((ident_bf, ident), (before_bf, cst[:, C_BEFORE:C_BEFORE + 128])):
                    nc.vector.tensor_copy(dst[:, :], src).then_inc(consts_made, 1)
                nc.vector.memset(ones_bf[:, :], 1.0).then_inc(consts_made, 1)
                nc.vector.memset(quarter[:, :], float(np.pi / 2))
                nc.vector.memset(eps[:, :], EPS)
                nc.vector.memset(causal1[:, :, 0:128], 0.0)
                nc.vector.memset(slot[:, :, :, :], 0.0)
                tri = cst[:, C_TRI:C_TRI + 128]
                for t in range(2):
                    nc.vector.tensor_copy(causal0[:, t], tri)
                    nc.vector.tensor_copy(causal1[:, t, 128:256], tri)
                dve.wait_ge(x_all_in, 64)
                stage = cs[:, :, :, :, :].rearrange("p q a b c -> p (q a b c)")
                with dve.Fori(0, B * NB // 8) as i:
                    for t in range(8):
                        tile = i * 8 + t
                        nc.vector.bn_stats(st[:, bass.ds(tile, 1), :].rearrange("p a b -> p (a b)"),
                                           stage[:, bass.ds(tile * 128, 128)]).then_inc(stats_read, 1)
                dve.wait_ge(stats_read, B * NB)
                c = [0]

                def step(ins):
                    c[0] += 1
                    ins.then_inc(norm_step, 1)
                    dve.wait_ge(norm_step, c[0])

                me, m2e, mo, m2o = st[:, :, 1], st[:, :, 2], st[:, :, 4], st[:, :, 5]
                tt(va[:, :], me, mo, ALU.subtract)
                step(tt(vb[:, :], m2e, m2o, ALU.add))
                step(tt(va[:, :], va[:, :], va[:, :], ALU.mult))
                step(tt(mean[:, :], me, mo, ALU.add))
                step(ts(mean[:, :], mean[:, :], 0.5, None, ALU.mult))
                step(stt(va[:, :], va[:, :], E / 4.0, vb[:, :], ALU.mult, ALU.add))
                ts(vb[:, :], va[:, :], 1.0 / E, None, ALU.mult).then_inc(norm_sync, 1)
                dve.wait_ge(norm_sync, 1)
                step(ts(va[:, :], vb[:, :], EPS, None, ALU.add))
                dve.wait_ge(std_ready, 1)
                step(nc.vector.reciprocal(rstd[:, :], vc[:, :]))
                step(tt(vb[:, :], rstd[:, :], rstd[:, :], ALU.mult))
                step(tt(vb[:, :], vb[:, :], va[:, :], ALU.mult))
                step(ts(vb[:, :], vb[:, :], -0.5, 1.5, ALU.mult, ALU.add))
                step(tt(rstd[:, :], rstd[:, :], vb[:, :], ALU.mult))
                norm(0, 0)
                for stage in (*range(11), 14, 15, 11, 12, 13):
                    route(0, 0, stage)
                for t in range(NG):
                    rounds(0, t)
                    if t >= 1:
                        absolutes(0, 0, t - 1)
                absolutes(0, 0, NG - 1)
                rotate(0, 0, 0)
                rotate(0, 0, 1)
                rotate(0, 1, 0)
                rotate(0, 1, 1)
                dve.wait_ge(weights_in, 16 * WEIGHT_LOADS)

            ROUTE = {2: (0, 1, 2, 3, 4), 3: (5, 6, 7, 8, 9), 4: (10, 14, 15), 5: (11, 12, 13)}

            def between(b, par, more, k, point):
                if 3 <= k < 3 + INNER // 2 and point in (1, 3):
                    gate(b, par, 2 * (k - 3) + point // 2)
                if k == 13 and not first(b):
                    if point == 0:
                        add_residual(b - 1, 1 - par)
                    if point == 2:
                        add_bias(b - 1, 1 - par)
                if more:
                    if k == 0 and point == 4:
                        norm(b + 1, 1 - par)
                    stages = ROUTE.get(k, ())
                    if point < len(stages):
                        route(b + 1, 1 - par, stages[point])
                    if 7 <= k < 7 + NG and point == 2:
                        rounds(b + 1, k - 7)
                    if 8 <= k < 8 + NG and point == 4:
                        absolutes(b + 1, 1 - par, k - 8)

            def steps(b, par, more):
                for k in range(NH + (0 if more else 2)):
                    lb, g, there = lagged(b, k, 2)
                    lpar = par if k >= 2 else 1 - par
                    if there:
                        invert(lb, g)
                    if k < NH:
                        negate(b, k, 0)
                    if there:
                        weigh(lb, g, lpar)
                    if k < NH:
                        negate(b, k, 1)
                        between(b, par, more, k, 0)
                        negate(b, k, 2)
                        between(b, par, more, k, 1)
                        for rb, hp, what in rotated(b, k, more):
                            rotate(rb, hp, what)
                        between(b, par, more, k, 2)
                    if there:
                        combine_low(lb, g)
                    if k < NH:
                        between(b, par, more, k, 3)
                    if there:
                        combine_high(lb, g)
                    if k < NH:
                        between(b, par, more, k, 4)

            body(dve, steps, prologue)
            add_residual(B - 1, (B - 1) % 2)
            add_bias(B - 1, (B - 1) % 2)

        @block.gpsimd
        def _(pool):
            tt = nc.gpsimd.tensor_tensor

            def part_turns(nb, par, t):
                pool.wait_ge(whole_made, NG * nb + t + 1)
                wait(pool, k_prod, HP * (nb - 1))
                tt(cs[:, par, t, 1, :], turns[:, t % 2], whole[:, t % 2], ALU.subtract).then_inc(frac_made, 1)

            def add_rotated(b, hp, what):
                H, r = b * HP + hp, hp % 2
                wait(pool, qk_in[r], 64 * (b * (HP // 2) + hp // 2))
                pool.wait_ge((q_prod, k_prod)[what], H + 1)
                tt(rot[:, r, what], prod[:, what, 0], prod[:, what, 1], ALU.add).then_inc(rot_made, 1)

            def add_slots(b, g):
                G, r = b * NH + g, g % 2
                pool.wait_ge(exp_made, 3 * G + 1)
                wait(pool, probs_made, G - 1)
                e = expd[:, r, 0].rearrange("p (s t j) -> p s t j", s=2, t=2)
                tt(sums[:, r, 0:256].rearrange("p (s j) -> p s j", s=2), e[:, :, 0], e[:, :, 1], ALU.add).then_inc(slots_added, 1)
                pool.wait_ge(exp_made, 3 * G + 3)
                tt(sums[:, r, 256:768].rearrange("p (s j) -> p s j", s=2), expd[:, r, 1:3, 0:256], expd[:, r, 1:3, 256:512],
                   ALU.add).then_inc(slots_added, 1)

            def prologue():
                nc.gpsimd.memset(wout_sb[:, :, :], 0.0).then_inc(zeroed, 1)
                nc.gpsimd.memset(qk[:, :, :, :, :], 0.0).then_inc(zeroed, 1)
                pool.wait_ge(weights_in, 16 * WEIGHT_LOADS)
                halves = lambda t: t.rearrange("p (h c f) -> p h c f", c=2, f=F)
                q_from, q_to = halves(wq_sb[:, :]), halves(wq_rot[:, :])
                nc.gpsimd.tensor_scalar(q_to[:, :, 0], q_from[:, :, 1], -1.0, None, ALU.mult).then_inc(weights_made, 1)
                nc.gpsimd.tensor_copy(q_to[:, :, 1], q_from[:, :, 0]).then_inc(weights_made, 1)
                k_from = halves(wk_in)
                both = lambda v: v.rearrange("p h (o f) -> p h o f", o=1).broadcast_to([128, NKV, 2, v.shape[-1]])
                nc.gpsimd.tensor_copy(wk_two[:, :, :, :], both(wk_in.rearrange("p (h d) -> p h d", h=NKV))).then_inc(weights_made, 1)
                nc.gpsimd.tensor_scalar(wk_rot[:, :, :, 0:F], both(k_from[:, :, 1]), -1.0, None, ALU.mult).then_inc(weights_made, 1)
                nc.gpsimd.tensor_copy(wk_rot[:, :, :, F:D], both(k_from[:, :, 0])).then_inc(weights_made, 1)
                for t in range(NG):
                    part_turns(0, 0, t)
                add_rotated(0, 0, 0)
                add_rotated(0, 0, 1)
                add_rotated(0, 1, 0)
                add_rotated(0, 1, 1)

            def steps(b, par, more):
                for k in range(NH + (0 if more else 1)):
                    lb, g, there = lagged(b, k, 1)
                    if there:
                        add_slots(lb, g)
                    if k < NH:
                        for rb, hp, what in rotated(b, k, more):
                            add_rotated(rb, hp, what)
                    if more and 7 <= k < 7 + NG:
                        part_turns(b + 1, 1 - par, k - 7)

            body(pool, steps, prologue)


_INS = ["L0_attn_x", "L0_attn_wq", "L0_attn_wk", "L0_attn_wv", "L0_attn_wr", "L0_attn_wo", "L0_ffn_Win", "L0_ffn_bin_",
        "L0_ffn_W1", "L0_ffn_b1", "L0_ffn_W2", "L0_ffn_b2", "L0_ffn_Wout", "L0_ffn_bout"]


def kernel(**inputs):
    import numpy as _np
    import concourse.bacc as _bacc
    from concourse import mybir as _mybir
    from concourse.bass_utils import run_bass_kernel_spmd as _run

    nc = _bacc.Bacc("TRN2", target_bir_lowering=False, num_devices=1)
    arrays, args = {}, []
    for name in _INS:
        a = _np.ascontiguousarray(inputs[name])
        arrays[f"in_{name}_dram"] = a
        args.append(nc.dram_tensor(f"in_{name}_dram", a.shape, _mybir.dt.from_np(a.dtype), kind="ExternalInput").ap())
    arrays["shape_constants"] = shape_constants()
    args.append(nc.dram_tensor("shape_constants", (128, C_COLS), _mybir.dt.float32, kind="ExternalInput").ap())
    args.append(nc.dram_tensor("out_0_dram", (B, N, E), _mybir.dt.float32, kind="ExternalOutput").ap())
    routed_attention_block(nc, *args)
    r = _run(nc, [arrays], core_ids=[0])
    return r.results[0]["out_0_dram"]
```

```python
import concourse.bass as bass
from concourse import mybir
from contextlib import ExitStack

import numpy as np

B, N, E = 32, 256, 128
NH, NKV, D, ND = 16, 4, 64, 4
HP = NH // 2
NB = N // 128
F = D // 2
GH = 128 // F
NG = NH // GH
M, INNER = 64, 16
SCALE = float(D) ** -0.5
BIG = 1.0e9
EPS = 1.0e-5
ROUND = 12582912.0
TURN = 6.283185
RING = 4
LAG = 3
TRIG_STEP = 12
C_ID, C_TRI, C_BEFORE, C_FREQ, C_COLS = 0, 128, 256, 384, 385


def shape_constants():
    c = np.zeros((128, C_COLS), np.float32)
    row, col = np.arange(128)[:, None], np.arange(128)[None, :]
    c[:, C_ID:C_ID + 128] = row == col
    c[:, C_TRI:C_TRI + 128] = np.where(col > row, -BIG, 0.0)
    c[:, C_BEFORE:C_BEFORE + 128] = row < col
    freq = 1.0 / 10000.0 ** (np.arange(0, D, 2, dtype=np.float64) / D)
    c[:, C_FREQ] = (freq / (2 * np.pi)).astype(np.float32)[np.arange(128) % F]
    return c


def routed_attention_block(nc, x, wq, wk, wv, wr, wo, Win, bin_, W1, b1, W2, b2, Wout, bout, consts, out):
    fp32, bf16 = mybir.dt.float32, mybir.dt.bfloat16
    ALU, ACT, AX = mybir.AluOpType, mybir.ActivationFunctionType, mybir.AxisListType

    ctx = ExitStack()
    with ctx:
        def sb(name, shape, dt=fp32):
            return ctx.enter_context(nc.sbuf_tensor(name, shape, dt))

        def sem(name):
            return ctx.enter_context(nc.semaphore(name))

        cst = sb("cst", [128, C_COLS])
        ident = cst[:, C_ID:C_ID + 128]
        ident_bf = sb("ident_bf", [128, 128], bf16)
        before_bf = sb("before_bf", [128, 128], bf16)
        ones_bf = sb("ones_bf", [128, 128], bf16)
        causal0 = sb("causal0", [128, 2, 128])
        causal1 = sb("causal1", [128, 2, 256])
        quarter = sb("quarter", [128, 1])
        eps = sb("eps", [128, 1])
        wq_sb = sb("wq_sb", [128, NH * D])
        wq_rot = sb("wq_rot", [128, NH * D])
        wk_two = sb("wk_two", [128, NKV, 2, D])
        wk_rot = sb("wk_rot", [128, NKV, 2, D])
        wv_sb = sb("wv_sb", [128, NKV * D])
        wr_sb = sb("wr_sb", [128, NH * ND])
        wo_sb = sb("wo_sb", [128, HP, E])
        win_sb = sb("win_sb", [128, M])
        wout_sb = sb("wout_sb", [128, NB, E])
        bin_sb = sb("bin_sb", [128, 1])
        b2_sb = sb("b2_sb", [128, 1])
        w1_sb = sb("w1_sb", [128, INNER])
        b1_sb = sb("b1_sb", [128, INNER])
        w2_sb = sb("w2_sb", [128, INNER])
        bout_sb = sb("bout_sb", [128, E])
        mean = sb("mean", [128, B * NB])
        rstd = sb("rstd", [128, B * NB])
        va, vb, vc = (sb(n, [128, B * NB]) for n in ("va", "vb", "vc"))
        x_ln = sb("x_ln", [128, 2, NB, E])
        x_out = sb("x_out", [128, 2, NB, E])
        xn = sb("xn", [128, NB, E])
        xnT = sb("xnT", [128, 2, N])
        lg = sb("lg", [128, NB * NH, ND])
        ge0 = sb("ge0", [128, NB * NH, 3])
        ge1 = sb("ge1", [128, NB * NH, 2])
        ge2 = sb("ge2", [128, NB * NH, 1])
        win = sb("win", [128, NB * NH, ND])
        mem = sb("mem", [128, NB * NH, ND])
        mem_bf = sb("mem_bf", [128, NB * NH, ND], bf16)
        low = sb("low", [128, NB * NH, 1])
        slot = sb("slot", [128, 2, NB * NH, ND])
        sel = sb("sel", [128, NB * NH, 2, ND])
        sv = sb("sv", [128, NB * NH, 2])
        se = sb("se", [128, NB * NH, 2])
        smax = sb("smax", [128, NB * NH, 1])
        ssum = sb("ssum", [128, NB * NH, 1])
        wslot = sb("wslot", [128, 2, NB, NH, 2])
        pos_bf = sb("pos_bf", [128, NB * NH, 2], bf16)
        code = sb("code", [64, 2, 2, 2 * N])
        turns = sb("turns", [128, 2, 2 * N])
        whole = sb("whole", [128, 2 * N])
        cs = sb("cs", [128, 2, NG, 2, 2 * N])
        pair_cs = sb("pair_cs", [128, 2, 2, 2 * N])
        prod = sb("prod", [128, 2, 2, 2 * N])
        rot = sb("rot", [128, 2, 2, 2 * N])
        qk = sb("qk", [128, 2, 2, 2, 2 * N])
        k_half = sb("k_half", [128, N])
        neg_s = sb("neg_s", [128, RING, 3, 512])
        neg_max = sb("neg_max", [128, RING, 4])
        expd = sb("expd", [128, 2, 3, 512])
        total = sb("total", [128, RING, 4])
        recip = sb("recip", [128, 2, 4])
        coef = sb("coef", [128, 2, 4])
        sums = sb("sums", [128, RING, 768])
        probs = sb("probs", [128, 2, 384])
        probsT = sb("probsT", [128, 2, 384])
        v_sb = sb("v_sb", [128, 2, NB, NKV * D])
        yT = sb("yT", [128, 2, HP, N])
        sT = sb("sT", [128, 2, 128])
        hT = sb("hT", [128, 4, 2, 128])
        g_sum = sb("g_sum", [128, 2, 128])
        gT = sb("gT", [128, 2, 128])

        wk_in = prod[:, 0, 0, 0:NKV * D]
        st = expd[:, 0, 0, 0:B * NB * 6].rearrange("p (t c) -> p t c", c=6)

        def pb(name):
            return ctx.enter_context(nc.psum_tensor(name, [128, 512], fp32))

        p_score = [pb(f"p_score{u}") for u in range(3)]
        p_q, p_k, p_misc, p_pt, p_y = (pb(n) for n in ("p_q", "p_k", "p_misc", "p_pt", "p_y"))

        consts_in, weights_in = sem("consts_in"), sem("weights_in")
        x_all_in, norm_step, std_ready = sem("x_all_in"), sem("norm_step"), sem("std_ready")
        norm_sync, weights_made, consts_made = sem("norm_sync"), sem("weights_made"), sem("consts_made")
        zeroed, stats_read = sem("zeroed"), sem("stats_read")
        x_ln_in = [sem("x_ln_in0"), sem("x_ln_in1")]
        x_out_in = [sem("x_out_in0"), sem("x_out_in1")]
        stored = [sem("stored0"), sem("stored1")]
        xn_made, xnT_mm, xnT_made = sem("xn_made"), sem("xnT_mm"), sem("xnT_made")
        logits_mm, logits_made, sT_made = sem("logits_mm"), sem("logits_made"), sem("sT_made")
        route_step, mem_made, slot_made, slot_exp = sem("route_step"), sem("mem_made"), sem("slot_made"), sem("slot_exp")
        diff_made, wslot_made = sem("diff_made"), sem("wslot_made")
        pos_mm, pos_sel, pos_made = sem("pos_mm"), sem("pos_sel"), sem("pos_made")
        code_mm, code_made = sem("code_mm"), sem("code_made")
        v_mm, v_made = sem("v_mm"), sem("v_made")
        turn_mm, turn_made, whole_made = sem("turn_mm"), sem("turn_made"), sem("whole_made")
        frac_made, abs_made, table_made = sem("frac_made"), sem("abs_made"), sem("table_made")
        q_mm, k_mm, q_prod, k_prod = sem("q_mm"), sem("k_mm"), sem("q_prod"), sem("k_prod")
        rot_made = sem("rot_made")
        qk_in = [sem("qk_in0"), sem("qk_in1")]
        first_table_made = sem("first_table_made")
        low_made = sem("low_made")
        k_kept, k_sin = sem("k_kept"), sem("k_sin")
        pair_cs_in = [sem("pair_cs_in0"), sem("pair_cs_in1")]
        score_mm, score_neg, exp_made, slots_added = sem("score_mm"), sem("score_neg"), sem("exp_made"), sem("slots_added")
        coef_step, probs_made, pt_mm, pt_made = sem("coef_step"), sem("probs_made"), sem("pt_mm"), sem("pt_made")
        y_mm, yT_made = sem("y_mm"), sem("yT_made")
        relu_made, g_step = sem("relu_made"), sem("g_step")
        pe_waited, dve_waited = sem("pe_waited"), sem("dve_waited")
        out_mm, out_read, out_made = sem("out_mm"), sem("out_read"), sem("out_made")

        WEIGHT_LOADS = 7 + 6 * NB

        x_tok = x.rearrange("b (n p) e -> p b n e", p=128)
        out_tok = out.rearrange("b (n p) e -> p b n e", p=128)

        def wait(eng, s, value):
            if not (isinstance(value, int) and value <= 0):
                eng.wait_ge(s, value)

        def first(b):
            return isinstance(b, int) and b == 0

        def loads_of(b, par):
            return b * 8 + (16 - 8 * par)

        def body(eng, steps, prologue):
            prologue()
            steps(0, 0, True)
            with eng.Fori(0, (B - 2) // 2) as i:
                steps(i * 2 + 1, 1, True)
                steps(i * 2 + 2, 0, True)
            steps(B - 1, 1, False)

        def sweeps_before(b):
            return 0 if first(b) else b * 8 + 8

        def sweep_of(b, par):
            return b * 8 + (24 if par else 16)

        def swept(b, par, more):
            return slice(0, 1) if first(b) else slice(0, 0) if par == 0 else slice(0 if more else 1, 2)

        assert INNER == 16

        SWEEP = {3: (0, 1), 4: (2, 3), 5: (4, 5), 6: (6, 7), **{k: (k + 1,) for k in range(7, 12)}, 12: (), 13: (13, 14), 14: (15,)}

        LOW_BY_VECTOR = (TRIG_STEP, TRIG_STEP + 1)

        def lagged(b, k, lag):
            g = k - lag
            if g < 0:
                return b - 1, g + NH, not first(b)
            return b, g, g < NH

        def rotated(b, k, more):
            parts = {NH - 4: [], NH - 3: [(HP, 0), (HP, 1)]}.get(k, [(k // 2 + 2, k % 2)])
            here = [(b, hp, what) for hp, what in parts if hp < HP]
            return here + [(b + 1, hp - HP, what) for hp, what in parts if hp >= HP and more]

        block = ctx.enter_context(nc.Block())

        @block.sync
        def _(sp):
            def load_ln(nb, par):
                wait(sp, xn_made, nb - 1)
                sp.dma_start(x_ln[:, par], x_tok[:, bass.ds(nb, 1)]).then_inc(x_ln_in[par], 16)

            def place(b, hp, par):
                H, r = b * HP + hp, hp % 2
                wait(sp, score_mm, 6 * H - 6)
                if hp == 0:
                    sp.wait_ge(code_made, 2 * b + 2)
                for h in range(2):
                    head = 2 * hp + h
                    c0 = 64 - 64 * h
                    sp.dma_start(qk[c0:c0 + ND, r, :, h, :], code[ND * head:ND * head + ND, par]).then_inc(qk_in[r], 16)
                wait(sp, rot_made, 2 * H + 2)
                for h in range(2):
                    sp.dma_start(qk[64 * h:64 * h + 64, r, :, h, :], rot[64 * h:64 * h + 64, r]).then_inc(qk_in[r], 16)

            def replicate(b, hp, par):
                H, r = b * HP + hp, hp % 2
                wait(sp, rot_made, 2 * H - 2)
                if hp == 0:
                    sp.wait_ge(first_table_made, 2 * b + 2)
                if hp == GH // 2:
                    sp.wait_ge(table_made, 2 * b + 2)
                for h in range(2):
                    rows = cs[64 * (hp % 2) + F * h:64 * (hp % 2) + F * h + F, par, hp // 2]
                    for half in range(2):
                        to = 64 * h + F * half
                        sp.dma_start(pair_cs[to:to + F, r], rows).then_inc(pair_cs_in[r], 16)

            def prologue():
                sp.dma_start(cst[:, :], consts).then_inc(consts_in, 16)
                stage = cs[:, :, :, :, :].rearrange("p q a b c -> p (q a b c)").rearrange("p (t n e) -> p t n e", t=B, n=NB)
                for q in range(4):
                    sp.dma_start(stage[:, 8 * q:8 * q + 8], x_tok[:, 8 * q:8 * q + 8]).then_inc(x_all_in, 16)
                sp.dma_start(wq_sb[:, :], wq).then_inc(weights_in, 16)
                sp.dma_start(wk_in, wk).then_inc(weights_in, 16)
                sp.dma_start(wv_sb[:, :], wv).then_inc(weights_in, 16)
                sp.dma_start(wr_sb[:, :], wr).then_inc(weights_in, 16)
                sp.dma_start(wo_sb[:, :, :], wo.rearrange("(h p) e -> p h e", p=128)).then_inc(weights_in, 16)
                sp.dma_start(win_sb[:, :], Win).then_inc(weights_in, 16)
                sp.dma_start(bout_sb[:, :], bout.rearrange("(o e) -> o e", o=1).broadcast_to([128, E])).then_inc(weights_in, 16)
                col = lambda v: v.rearrange("(m o) -> m o", o=1)
                for blk in range(NB):
                    rows = slice(64 * blk, 64 * blk + 64)
                    for dst, src in ((w1_sb, W1), (b1_sb, b1), (w2_sb, W2)):
                        sp.dma_start(dst[rows, :], src).then_inc(weights_in, 16)
                    sp.dma_start(bin_sb[rows, :], col(bin_)).then_inc(weights_in, 16)
                    sp.dma_start(b2_sb[rows, :], col(b2)).then_inc(weights_in, 16)
                load_ln(0, 0)
                sp.dma_start(x_out[:, 0], x_tok[:, 0:1]).then_inc(x_out_in[0], 16)
                sp.wait_ge(zeroed, 2)
                for blk in range(NB):
                    sp.dma_start(wout_sb[64 * blk:64 * blk + 64, blk, :], Wout).then_inc(weights_in, 16)
                replicate(0, 0, 0)
                replicate(0, 1, 0)
                place(0, 0, 0)
                replicate(0, 2, 0)
                place(0, 1, 0)

            def steps(b, par, more):
                for k in range(NH):
                    if k == 0 and more:
                        load_ln(b + 1, 1 - par)
                    if k == NH - 1:
                        if not first(b):
                            sp.wait_ge(out_made, b)
                            sp.dma_start(out_tok[:, bass.ds(b - 1, 1)], x_out[:, 1 - par]).then_inc(stored[1 - par], 16)
                        if more:
                            if not first(b):
                                sp.wait_ge(stored[1 - par], loads_of(b - 1, 1 - par))
                            sp.dma_start(x_out[:, 1 - par], x_tok[:, bass.ds(b + 1, 1)]).then_inc(x_out_in[1 - par], 16)
                    if k % 2 == 1:
                        ahead = (k + 5) // 2
                        if ahead < HP:
                            replicate(b, ahead, par)
                        elif more and ahead > HP:
                            replicate(b + 1, ahead - HP, 1 - par)
                        now = (k + 3) // 2
                        if now < HP:
                            place(b, now, par)
                        elif more:
                            place(b + 1, now - HP, 1 - par)
                    if k == NH - 4 and more:
                        replicate(b + 1, 0, 1 - par)

            body(sp, steps, prologue)
            sp.wait_ge(out_made, B)
            sp.dma_start(out_tok[:, B - 1:B], x_out[:, (B - 1) % 2]).then_inc(stored[(B - 1) % 2], 16)
            sp.wait_ge(stored[0], 16 * (B // 2))
            sp.wait_ge(stored[1], 16 * (B // 2))

        @block.tensor
        def _(pe):
            mm = nc.tensor.matmul

            def transpose_x(nb, par):
                pe.wait_ge(xn_made, nb + 1)
                wait(pe, out_read, nb - 2)
                if isinstance(nb, int) and nb == 1:
                    pe.wait_ge(v_made, 1)
                for blk in range(NB):
                    last = nc.tensor.transpose(p_misc[:, 128 * blk:128 * blk + 128], xn[:, blk, :], ident)
                last.then_inc(xnT_mm, 1)

            def logits(nb, par):
                pe.wait_ge(xnT_made, nb + 1)
                for blk in range(NB):
                    mm(p_misc[:, 64 * blk:64 * blk + 64], xnT[:, par, 128 * blk:128 * blk + 128], wr_sb[:, :],
                       start=True, stop=True)
                for blk in range(NB):
                    last = mm(p_misc[64 * blk:64 * blk + 64, 128:256], win_sb[:, :],
                              xnT[:, par, 128 * blk:128 * blk + 128], start=True, stop=True)
                last.then_inc(logits_mm, 1)

            def values(nb, par):
                pe.wait_ge(turn_made, NG * (nb + 1))
                for blk in range(NB):
                    last = mm(p_misc[:, 256 * blk:256 * blk + 256], xnT[:, par, 128 * blk:128 * blk + 128],
                              wv_sb[:, :], start=True, stop=True)
                last.then_inc(v_mm, 1)

            def positions(nb, par):
                pe.wait_ge(mem_made, nb + 1)
                pe.wait_ge(logits_made, nb + 1)
                pe.wait_ge(sT_made, nb + 1)
                m = mem_bf[:, :, :].rearrange("p (n h) d -> p n (h d)", n=NB)
                mm(p_misc[:, 0:64], before_bf[:, :], m[:, 0], start=True, stop=True)
                mm(p_misc[:, 64:128], ones_bf[:, :], m[:, 0], start=True, stop=False)
                mm(p_misc[:, 64:128], before_bf[:, :], m[:, 1], start=False, stop=True).then_inc(pos_mm, 1)

            def codes(nb, par):
                pe.wait_ge(slot_made, nb + 1)
                pe.wait_ge(pos_sel, nb + 1)
                pe.sem_inc(pe_waited, 1)
                for s in range(2):
                    for blk in range(NB):
                        at = 256 * s + 128 * blk
                        last = nc.tensor.transpose(p_misc[0:64, at:at + 128], slot[:, s, NH * blk:NH * blk + NH, :].rearrange("p h d -> p (h d)"), ident)
                last.then_inc(code_mm, 1)

            def turn(nb, t):
                if t == 0:
                    pe.wait_ge(pos_made, nb + 1)
                    pe.wait_ge(code_made, 2 * nb + 2)
                wait(pe, turn_made, NG * nb + t)
                for s in range(2):
                    for blk in range(NB):
                        at = 256 * s + 128 * blk
                        for h in range(GH):
                            one = pos_bf[:, NH * blk + GH * t + h, s:s + 1].broadcast_to([128, F])
                            last = mm(p_misc[F * h:F * h + F, at:at + 128], one, ident_bf[:, :], start=True, stop=True)
                last.then_inc(turn_mm, 1)

            def project_q(b, hp, par):
                pe.wait_ge(xnT_made, b + 1)
                wait(pe, q_prod, b * HP + hp)
                mm(p_q[:, 0:256], wq_sb[:, 128 * hp:128 * hp + 128], xnT[:, par], start=True, stop=True)
                mm(p_q[:, 256:512], wq_rot[:, 128 * hp:128 * hp + 128], xnT[:, par], start=True, stop=True).then_inc(q_mm, 1)

            def project_k(b, hp, par):
                wait(pe, k_prod, b * HP + hp)
                wait(pe, k_kept, b * (HP // 2) + hp // 2)
                kv = hp // 2
                mm(p_k[:, 0:256], wk_two[:, kv].rearrange("p a d -> p (a d)"), xnT[:, par], start=True, stop=True)
                mm(p_k[:, 256:512], wk_rot[:, kv].rearrange("p a d -> p (a d)"), xnT[:, par],
                   start=True, stop=True).then_inc(k_mm, 1)

            def scores(b, g):
                G, h, r = b * NH + g, g % 2, (g // 2) % 2
                H_in_ring = b * (HP // 2) + g // 4
                if h == 0:
                    pe.wait_ge(qk_in[r], 64 * H_in_ring + 64)
                q, key = qk[:, r, 0, h, :], qk[:, r, 1, h, :].rearrange("p (t j) -> p t j", t=2)
                wait(pe, score_neg, 3 * G - 2)
                for s in range(2):
                    last = mm(p_score[0][:, 256 * s:256 * s + 256], q[:, 256 * s:256 * s + 128], key[:, :, 0:128],
                              start=True, stop=True)
                last.then_inc(score_mm, 1)
                for s in range(2):
                    wait(pe, score_neg, 3 * G - 1 + s)
                    mm(p_score[1 + s][:, :], q[:, 256 * s + 128:256 * s + 256], key, start=True, stop=True).then_inc(score_mm, 1)

            def transpose_probs(b, g):
                G = b * NH + g
                pe.wait_ge(probs_made, G + 1)
                wait(pe, pt_made, G)
                for j in range(3):
                    last = nc.tensor.transpose(p_pt[:, 128 * j:128 * j + 128], probs[:, g % 2, 128 * j:128 * j + 128], ident)
                last.then_inc(pt_mm, 1)

            def mix_values(b, g, par):
                G, h, kv = b * NH + g, g % 2, g // (NH // NKV)
                pe.wait_ge(pt_made, G + 1)
                pe.wait_ge(v_made, b + 1)
                if h == 0:
                    wait(pe, yT_made, b * HP + g // 2)
                rows, vs = slice(64 * h, 64 * h + 64), slice(D * kv, D * kv + D)
                mm(p_y[rows, 0:256], v_sb[:, par, 0, vs], probsT[:, g % 2, 0:256], start=True, stop=False)
                mm(p_y[rows, 128:256], v_sb[:, par, 1, vs], probsT[:, g % 2, 256:384], start=False, stop=True).then_inc(y_mm, 1)

            def project_out(b, par, blk):
                pe.wait_ge(yT_made, HP * b + HP)
                pe.wait_ge(g_step, sweep_of(b, par))
                o = p_misc[:, 128 * blk:128 * blk + 128]
                for hp in range(HP):
                    mm(o, yT[:, par, hp, 128 * blk:128 * blk + 128], wo_sb[:, hp, :], start=(hp == 0), stop=False)
                mm(o, gT[:, par, :], wout_sb[:, blk, :], start=False, stop=True).then_inc(out_mm, 1)

            def prologue():
                pe.wait_ge(consts_in, 16)
                pe.wait_ge(consts_made, 3)
                pe.wait_ge(weights_in, 16 * WEIGHT_LOADS)
                pe.wait_ge(weights_made, 5)
                transpose_x(0, 0)
                logits(0, 0)
                positions(0, 0)
                codes(0, 0)
                for t in range(NG):
                    turn(0, t)
                values(0, 0)
                project_q(0, 0, 0)
                project_k(0, 0, 0)
                project_q(0, 1, 0)
                project_q(0, 2, 0)

            def steps(b, par, more):
                for k in range(NH + (0 if more else LAG + 2)):
                    if k < NH:
                        scores(b, k)
                    if k < NH and k % 2 == 1:
                        hp = (k + 5) // 2
                        if hp < HP:
                            project_q(b, hp, par)
                        elif more and hp != HP + 1:
                            project_q(b + 1, hp - HP, 1 - par)
                    if more and k == NH - 2:
                        project_q(b + 1, 1, 1 - par)
                    if k < NH and k % 4 == 0:
                        hp = k // 2 + 2
                        if hp < HP:
                            project_k(b, hp, par)
                        elif more:
                            project_k(b + 1, 0, 1 - par)
                    lb, g, there = lagged(b, k, LAG + 1)
                    if there:
                        transpose_probs(lb, g)
                    lb, g, there = lagged(b, k, LAG + 2)
                    if there:
                        mix_values(lb, g, par if k >= LAG + 2 else 1 - par)
                    if more and k == 1:
                        transpose_x(b + 1, 1 - par)
                    if more and k == 2:
                        logits(b + 1, 1 - par)
                    if more and k == 4:
                        positions(b + 1, 1 - par)
                    if more and k == 5:
                        codes(b + 1, 1 - par)
                    if more and 6 <= k < 6 + NG:
                        turn(b + 1, k - 6)
                    if more and k == 10:
                        values(b + 1, 1 - par)
                    if k == 11 and not first(b):
                        if more:
                            pe.wait_ge(v_made, b + 2)
                        else:
                            pe.wait_ge(out_read, b - 1)
                        project_out(b - 1, 1 - par, 0)
                    if k == 12 and not first(b):
                        project_out(b - 1, 1 - par, 1)

            body(pe, steps, prologue)
            pe.wait_ge(out_read, B - 1)
            for blk in range(NB):
                project_out(B - 1, (B - 1) % 2, blk)

        @block.scalar
        def _(act):
            fn = nc.scalar.activation

            def keep_xT(nb, par):
                act.wait_ge(xnT_mm, nb + 1)
                wait(act, q_mm, HP * (nb - 1))
                fn(xnT[:, par], p_misc[:, 0:256], ACT.Copy).then_inc(xnT_made, 1)

            def keep_logits(nb, par):
                act.wait_ge(logits_mm, nb + 1)
                wait(act, wslot_made, nb)
                if not (isinstance(nb, int) and nb <= 1):
                    act.wait_ge(relu_made, sweep_of(nb - 2, par))
                fn(lg[:, :, :].rearrange("p a d -> p (a d)"), p_misc[:, 0:128], ACT.Copy).then_inc(logits_made, 1)
                fn(sT[:, par], p_misc[:, 128:256], ACT.Identity, bias=bin_sb[:, 0:1]).then_inc(sT_made, 1)

            def keep_values(nb, par):
                act.wait_ge(v_mm, nb + 1)
                wait(act, y_mm, NH * (nb - 1))
                fn(v_sb[:, par].rearrange("p n d -> p (n d)"), p_misc[:, :], ACT.Copy).then_inc(v_made, 1)

            def slot_exps(nb):
                act.wait_ge(diff_made, nb + 1)
                wait(act, wslot_made, nb)
                fn(se[:, :, :], sv[:, :, :], ACT.Exp).then_inc(slot_exp, 1)

            def keep_codes(nb, par):
                act.wait_ge(code_mm, nb + 1)
                for r in range(2):
                    wait(act, qk_in[r], 64 * (HP // 2) * (nb - 1))
                fn(code[:, par, 0, :], p_misc[0:64, :], ACT.Copy, scale=-1.0, bias=1.0).then_inc(code_made, 1)
                fn(code[:, par, 1, :], p_misc[0:64, :], ACT.Copy, scale=-BIG).then_inc(code_made, 1)

            def keep_turns(nb, t):
                act.wait_ge(turn_mm, NG * nb + t + 1)
                wait(act, frac_made, NG * nb + t - 1)
                fn(turns[:, t % 2], p_misc[:, :], ACT.Copy, scale=cst[:, C_FREQ:C_FREQ + 1]).then_inc(turn_made, 1)

            def trig(nb, par):
                act.wait_ge(abs_made, NG * (nb + 1))
                for groups, done in ((slice(0, 1), first_table_made), (slice(1, NG), table_made)):
                    cos, sin = cs[:, par, groups, 0, :], cs[:, par, groups, 1, :]
                    fn(cos, cos, ACT.Sin, bias=quarter[:, 0:1], scale=-TURN).then_inc(done, 1)
                    fn(sin, sin, ACT.Sin, scale=TURN).then_inc(done, 1)

            def relu(b, swept_now, j):
                if j == 0:
                    act.wait_ge(sT_made, b + swept_now.stop - swept_now.start)
                wait(act, g_step, sweeps_before(b) + j - 3)
                fn(hT[:, j % 4, swept_now], sT[:, swept_now], ACT.Relu, bias=b1_sb[:, j:j + 1], scale=w1_sb[:, j:j + 1]).then_inc(relu_made, 1)

            def exps(b, g):
                G, r = b * NH + g, g % 2
                act.wait_ge(score_neg, 3 * G + 1)
                wait(act, slots_added, 2 * G - 3)
                wait(act, coef_step, 2 * (G - RING) + 1)
                for s in range(2):
                    last = fn(expd[:, r, 0, 256 * s:256 * s + 256], neg_s[:, g % RING, 0, 256 * s:256 * s + 256], ACT.Exp,
                              bias=neg_max[:, g % RING, s:s + 1], scale=-1.0, accum_out=total[:, g % RING, s:s + 1])
                last.then_inc(exp_made, 1)
                wait(act, slots_added, 2 * G - 2)
                for s in range(2):
                    act.wait_ge(score_neg, 3 * G + 2 + s)
                    fn(expd[:, r, 1 + s, :], neg_s[:, g % RING, 1 + s, :], ACT.Exp, bias=neg_max[:, g % RING, 2 + s:3 + s], scale=-1.0,
                       accum_out=total[:, g % RING, 2 + s:3 + s]).then_inc(exp_made, 1)

            def keep_probsT(b, g):
                G = b * NH + g
                act.wait_ge(pt_mm, G + 1)
                wait(act, y_mm, G - 1)
                fn(probsT[:, g % 2], p_pt[:, 0:384], ACT.Copy).then_inc(pt_made, 1)

            def scale_low(b, g):
                G, r = b * NH + g, g % 2
                act.wait_ge(coef_step, 2 * G + 2)
                act.wait_ge(slots_added, 2 * G + 2)
                wait(act, pt_mm, G - 1)
                fn(probs[:, r, 0:128], sums[:, g % RING, 0:128], ACT.Copy, scale=coef[:, r, 0:1]).then_inc(low_made, 1)
                fn(probs[:, r, 128:384], sums[:, g % RING, 256:512], ACT.Copy, scale=coef[:, r, 2:3]).then_inc(low_made, 1)

            def keep_k_half(b, hp):
                act.wait_ge(k_mm, b * (HP // 2) + hp // 2 + 1)
                wait(act, k_sin, b * HP + hp)
                fn(k_half[:, :], p_k[:, 256:512], ACT.Copy).then_inc(k_kept, 1)

            def keep_yT(b, hp, par):
                act.wait_ge(y_mm, 2 * (b * HP + hp) + 2)
                if hp == 0:
                    wait(act, out_mm, NB * (b - 1))
                fn(yT[:, par, hp], p_y[:, 0:256], ACT.Copy).then_inc(yT_made, 1)

            def prologue():
                act.wait_ge(norm_sync, 1)
                fn(vc[:, :], vb[:, :], ACT.Sqrt, bias=eps[:, 0:1]).then_inc(std_ready, 1)
                keep_xT(0, 0)
                keep_logits(0, 0)
                slot_exps(0)
                keep_codes(0, 0)
                for t in range(NG):
                    keep_turns(0, t)
                keep_values(0, 0)
                trig(0, 0)
                keep_k_half(0, 0)

            def steps(b, par, more):
                for k in range(NH + (0 if more else LAG + 2)):
                    if more and k == 6:
                        slot_exps(b + 1)
                    if more and k == TRIG_STEP:
                        trig(b + 1, 1 - par)
                    lb, g, there = lagged(b, k, 1)
                    if there:
                        exps(lb, g)
                    lb, g, there = lagged(b, k, LAG)
                    if there and not (more and k in LOW_BY_VECTOR):
                        scale_low(lb, g)
                    lb, g, there = lagged(b, k, LAG + 1)
                    if there:
                        keep_probsT(lb, g)
                    lb, g, there = lagged(b, k, LAG + 2)
                    if there and g % 2 == 1:
                        keep_yT(lb, g // 2, par if k >= LAG + 2 else 1 - par)
                    if k < NH and k % 4 == 0:
                        hp = k // 2 + 2
                        if hp < HP:
                            keep_k_half(b, hp)
                        elif more:
                            keep_k_half(b + 1, 0)
                    if swept(b, par, more).stop:
                        for j in SWEEP.get(k, ()):
                            relu(b, swept(b, par, more), j)
                    if not more:
                        continue
                    if k == 1:
                        keep_xT(b + 1, 1 - par)
                    if k == 2:
                        keep_logits(b + 1, 1 - par)
                    if k == 10:
                        keep_values(b + 1, 1 - par)
                    if k == 5:
                        keep_codes(b + 1, 1 - par)
                    if 6 <= k < 6 + NG:
                        keep_turns(b + 1, k - 6)

            body(act, steps, prologue)

        @block.vector
        def _(dve):
            tt, ts, stt = nc.vector.tensor_tensor, nc.vector.tensor_scalar, nc.vector.scalar_tensor_tensor
            lgv = lg[:, :, :]

            def norm(nb, par):
                dve.wait_ge(x_ln_in[par], loads_of(nb, par))
                wait(dve, xnT_mm, nb)
                for blk in range(NB):
                    t = nb * NB + blk
                    last = ts(xn[:, blk, :], x_ln[:, par, blk, :], mean[:, bass.ds(t, 1)], rstd[:, bass.ds(t, 1)],
                              ALU.subtract, ALU.mult)
                last.then_inc(xn_made, 1)

            def route(nb, par, stage):
                if stage == 0:
                    dve.wait_ge(logits_made, nb + 1)
                    wait(dve, pos_mm, nb)
                    wait(dve, code_mm, nb)
                elif stage == 11:
                    dve.wait_ge(slot_exp, nb + 1)
                elif stage == 14:
                    dve.wait_ge(pos_mm, nb + 1)
                elif stage == 15:
                    dve.wait_ge(pos_sel, nb + 1)
                else:
                    dve.wait_ge(route_step, 12 * nb + (stage if stage <= 10 else stage - 1))
                l = lambda a, b_: lgv[:, :, a:b_]
                if stage == 0:
                    tt(ge0[:, :, :], l(0, 1).broadcast_to([128, NB * NH, 3]), l(1, 4), ALU.is_ge)
                    tt(ge1[:, :, :], l(1, 2).broadcast_to([128, NB * NH, 2]), l(2, 4), ALU.is_ge)
                    tt(ge2[:, :, :], l(2, 3), l(3, 4), ALU.is_ge).then_inc(route_step, 1)
                elif stage == 1:
                    tt(win[:, :, 0:1], ge0[:, :, 0:1], ge0[:, :, 1:2], ALU.add)
                    tt(win[:, :, 1:2], ge1[:, :, 0:1], ge1[:, :, 1:2], ALU.add)
                    tt(win[:, :, 2:4], ge0[:, :, 1:3], ge1[:, :, :], ALU.add).then_inc(route_step, 1)
                elif stage == 2:
                    tt(win[:, :, 0:1], win[:, :, 0:1], ge0[:, :, 2:3], ALU.add)
                    tt(win[:, :, 1:2], win[:, :, 1:2], ge0[:, :, 0:1], ALU.subtract)
                    tt(win[:, :, 2:3], win[:, :, 2:3], ge2[:, :, :], ALU.subtract)
                    tt(win[:, :, 3:4], win[:, :, 3:4], ge2[:, :, :], ALU.add).then_inc(route_step, 1)
                elif stage == 3:
                    for n, (op, bound) in enumerate(((ALU.is_ge, 2.0), (ALU.is_ge, 1.0), (ALU.is_le, 0.0), (ALU.is_le, 1.0))):
                        last = ts(mem[:, :, n:n + 1], win[:, :, n:n + 1], bound, None, op)
                    last.then_inc(route_step, 1)
                elif stage == 4:
                    nc.vector.tensor_copy(mem_bf[:, :, :], mem[:, :, :]).then_inc(mem_made, 1)
                    nc.vector.tensor_copy(slot[:, 0, :, 0:1], mem[:, :, 0:1])
                    tt(slot[:, 0, :, 1:2], mem[:, :, 1:2], mem[:, :, 0:1], ALU.is_gt)
                    tt(low[:, :, :], mem[:, :, 0:1], mem[:, :, 1:2], ALU.add).then_inc(route_step, 1)
                elif stage == 5:
                    tt(slot[:, 0, :, 2:3], mem[:, :, 2:3], low[:, :, :], ALU.is_gt).then_inc(route_step, 1)
                elif stage == 6:
                    tt(slot[:, 1], mem[:, :, :], slot[:, 0], ALU.subtract).then_inc(route_step, 1)
                elif stage == 7:
                    tt(sel[:, :, 0, :], slot[:, 0], lgv, ALU.mult).then_inc(slot_made, 1)
                    tt(sel[:, :, 1, :], slot[:, 1], lgv, ALU.mult).then_inc(route_step, 1)
                elif stage == 8:
                    nc.vector.tensor_reduce(sv[:, :, :], sel[:, :, :, :], AX.X, ALU.add).then_inc(route_step, 1)
                elif stage == 9:
                    tt(smax[:, :, :], sv[:, :, 0:1], sv[:, :, 1:2], ALU.max).then_inc(route_step, 1)
                elif stage == 10:
                    tt(sv[:, :, :], sv[:, :, :], smax[:, :, :].broadcast_to([128, NB * NH, 2]), ALU.subtract).then_inc(diff_made, 1)
                elif stage == 11:
                    tt(ssum[:, :, :], se[:, :, 0:1], se[:, :, 1:2], ALU.add).then_inc(route_step, 1)
                elif stage == 12:
                    nc.vector.reciprocal(ssum[:, :, :], ssum[:, :, :]).then_inc(route_step, 1)
                elif stage == 13:
                    w = wslot[:, par].rearrange("p n h s -> p (n h) s")
                    tt(w, se[:, :, :], ssum[:, :, :].broadcast_to([128, NB * NH, 2]), ALU.mult).then_inc(wslot_made, 1)
                elif stage == 14:
                    pos = p_misc[:, 0:128].rearrange("p (a d) -> p a d", d=ND)
                    tt(sel[:, :, 0, :], pos, slot[:, 0], ALU.mult)
                    tt(sel[:, :, 1, :], pos, slot[:, 1], ALU.mult).then_inc(pos_sel, 1)
                elif stage == 15:
                    with nc.allow_low_precision(reason="positions are integers below 256, exact in bf16"):
                        nc.vector.tensor_reduce(pos_bf[:, :, :], sel[:, :, :, :], AX.X, ALU.add).then_inc(pos_made, 1)

            def rounds(nb, t):
                dve.wait_ge(turn_made, NG * nb + t + 1)
                wait(dve, frac_made, NG * nb + t)
                ts(whole[:, :], turns[:, t % 2], ROUND, -ROUND, ALU.add, ALU.add).then_inc(whole_made, 1)

            def absolutes(nb, par, t):
                dve.wait_ge(frac_made, NG * nb + t + 1)
                stt(cs[:, par, t, 0, :], cs[:, par, t, 1, :], -1.0, cs[:, par, t, 1, :], ALU.mult, ALU.max).then_inc(abs_made, 1)

            def rotate(b, hp, what):
                H = b * HP + hp
                dve.wait_ge(pair_cs_in[hp % 2], 64 * (b * (HP // 2) + hp // 2 + 1))
                table = pair_cs[:, hp % 2].rearrange("p c (s i) -> p c s i", s=2)
                if what == 0:
                    dve.wait_ge(q_mm, H + 1)
                else:
                    dve.wait_ge(k_mm, b * (HP // 2) + hp // 2 + 1)
                    dve.wait_ge(k_kept, b * (HP // 2) + hp // 2 + 1)
                wait(dve, rot_made, 2 * H - 1 + what)
                bank, prod_done = ((p_q, q_prod), (p_k, k_prod))[what]
                for c in range(2 - what):
                    last = tt(prod[:, what, c].rearrange("p (s i) -> p s i", s=2),
                              bank[:, 256 * c:256 * c + 256].rearrange("p (o i) -> p o i", o=1).broadcast_to([128, 2, N]),
                              table[:, c], ALU.mult)
                last.then_inc(prod_done, 1)

            def negate(b, g, unit):
                G, r = b * NH + g, g % 2
                ttr = nc.vector.tensor_tensor_reduce
                dve.wait_ge(score_mm, 3 * G + 1 + unit)
                wait(dve, exp_made, 3 * (G - RING) + 1 + unit)
                dve.sem_inc(dve_waited, 1)
                if unit == 0:
                    for s in range(2):
                        cols = slice(256 * s, 256 * s + 256)
                        last = ttr(out=neg_s[:, g % RING, 0, cols], in0=p_score[0][:, cols], in1=causal0[:, :, :].rearrange("p t j -> p (t j)"),
                                   scale=-SCALE, scalar=3.0e38, op0=ALU.add, op1=ALU.min, accum_out=neg_max[:, g % RING, s:s + 1])
                else:
                    last = ttr(out=neg_s[:, g % RING, unit, :], in0=p_score[unit][:, :], in1=causal1[:, :, :].rearrange("p t j -> p (t j)"),
                               scale=-SCALE, scalar=3.0e38, op0=ALU.add, op1=ALU.min,
                               accum_out=neg_max[:, g % RING, 1 + unit:2 + unit])
                last.then_inc(score_neg, 1)

            def invert(b, g):
                dve.wait_ge(exp_made, 3 * (b * NH + g) + 3)
                nc.vector.reciprocal(recip[:, g % 2], total[:, g % RING]).then_inc(coef_step, 1)

            def weigh(b, g, par):
                dve.wait_ge(coef_step, 2 * (b * NH + g) + 1)
                tt(coef[:, g % 2].rearrange("p (n s) -> p n s", n=NB), wslot[:, par, :, g, :],
                   recip[:, g % 2].rearrange("p (n s) -> p n s", n=NB), ALU.mult).then_inc(coef_step, 1)

            def scale_low(b, g):
                G, r = b * NH + g, g % 2
                dve.wait_ge(coef_step, 2 * G + 2)
                dve.wait_ge(slots_added, 2 * G + 2)
                wait(dve, pt_mm, G - 1)
                ts(probs[:, r, 0:128], sums[:, g % RING, 0:128], coef[:, r, 0:1], None, ALU.mult).then_inc(low_made, 1)
                ts(probs[:, r, 128:384], sums[:, g % RING, 256:512], coef[:, r, 2:3], None, ALU.mult).then_inc(low_made, 1)

            def combine(b, g):
                G, r = b * NH + g, g % 2
                p0, p1 = probs[:, r, 0:128], probs[:, r, 128:384]
                dve.wait_ge(low_made, 2 * G + 2)
                stt(p0, sums[:, g % RING, 128:256], coef[:, r, 1:2], p0, ALU.mult, ALU.add)
                stt(p1, sums[:, g % RING, 512:768], coef[:, r, 3:4], p1, ALU.mult, ALU.add).then_inc(probs_made, 1)

            def gate(b, swept_now, j):
                steps = sweeps_before(b)
                dve.wait_ge(relu_made, steps + j + 1)
                wait(dve, g_step, steps + j)
                if j == INNER - 1:
                    wait(dve, out_mm, NB * b)
                total_g = g_sum if j < INNER - 1 else gT
                if j == 0:
                    ins = ts(total_g[:, swept_now], hT[:, 0, swept_now], w2_sb[:, 0:1], b2_sb[:, 0:1], ALU.mult, ALU.add)
                else:
                    ins = stt(total_g[:, swept_now], hT[:, j % 4, swept_now], w2_sb[:, j:j + 1], g_sum[:, swept_now],
                              ALU.mult, ALU.add)
                ins.then_inc(g_step, 1)

            def add_residual(b, par):
                dve.wait_ge(out_mm, NB * (b + 1))
                dve.wait_ge(x_out_in[par], loads_of(b, par))
                tt(x_out[:, par], p_misc[:, 0:256].rearrange("p (n e) -> p n e", n=NB), x_out[:, par], ALU.add).then_inc(out_read, 1)

            def add_bias(b, par):
                dve.wait_ge(out_read, b + 1)
                for blk in range(NB):
                    last = tt(x_out[:, par, blk, :], x_out[:, par, blk, :], bout_sb[:, :], ALU.add)
                last.then_inc(out_made, 1)

            def prologue():
                dve.wait_ge(consts_in, 16)
                for dst, src in ((ident_bf, ident), (before_bf, cst[:, C_BEFORE:C_BEFORE + 128])):
                    nc.vector.tensor_copy(dst[:, :], src).then_inc(consts_made, 1)
                nc.vector.memset(ones_bf[:, :], 1.0).then_inc(consts_made, 1)
                nc.vector.memset(quarter[:, :], float(np.pi / 2))
                nc.vector.memset(eps[:, :], EPS)
                nc.vector.memset(causal1[:, :, 0:128], 0.0)
                nc.vector.memset(slot[:, :, :, :], 0.0)
                tri = cst[:, C_TRI:C_TRI + 128]
                for t in range(2):
                    nc.vector.tensor_copy(causal0[:, t], tri)
                    nc.vector.tensor_copy(causal1[:, t, 128:256], tri)
                dve.wait_ge(x_all_in, 64)
                stage = cs[:, :, :, :, :].rearrange("p q a b c -> p (q a b c)")
                with dve.Fori(0, B * NB // 8) as i:
                    for t in range(8):
                        tile = i * 8 + t
                        nc.vector.bn_stats(st[:, bass.ds(tile, 1), :].rearrange("p a b -> p (a b)"),
                                           stage[:, bass.ds(tile * 128, 128)]).then_inc(stats_read, 1)
                dve.wait_ge(stats_read, B * NB)
                c = [0]

                def step(ins):
                    c[0] += 1
                    ins.then_inc(norm_step, 1)
                    dve.wait_ge(norm_step, c[0])

                me, m2e, mo, m2o = st[:, :, 1], st[:, :, 2], st[:, :, 4], st[:, :, 5]
                tt(va[:, :], me, mo, ALU.subtract)
                step(tt(vb[:, :], m2e, m2o, ALU.add))
                step(tt(va[:, :], va[:, :], va[:, :], ALU.mult))
                step(tt(mean[:, :], me, mo, ALU.add))
                step(ts(mean[:, :], mean[:, :], 0.5, None, ALU.mult))
                step(stt(va[:, :], va[:, :], E / 4.0, vb[:, :], ALU.mult, ALU.add))
                ts(vb[:, :], va[:, :], 1.0 / E, None, ALU.mult).then_inc(norm_sync, 1)
                dve.wait_ge(norm_sync, 1)
                step(ts(va[:, :], vb[:, :], EPS, None, ALU.add))
                dve.wait_ge(std_ready, 1)
                step(nc.vector.reciprocal(rstd[:, :], vc[:, :]))
                step(tt(vb[:, :], rstd[:, :], rstd[:, :], ALU.mult))
                step(tt(vb[:, :], vb[:, :], va[:, :], ALU.mult))
                step(ts(vb[:, :], vb[:, :], -0.5, 1.5, ALU.mult, ALU.add))
                step(tt(rstd[:, :], rstd[:, :], vb[:, :], ALU.mult))
                norm(0, 0)
                for stage in (*range(11), 14, 15, 11, 12, 13):
                    route(0, 0, stage)
                for t in range(NG):
                    rounds(0, t)
                    if t >= 1:
                        absolutes(0, 0, t - 1)
                absolutes(0, 0, NG - 1)
                rotate(0, 0, 0)
                rotate(0, 0, 1)
                rotate(0, 1, 0)
                rotate(0, 1, 1)
                dve.wait_ge(weights_in, 16 * WEIGHT_LOADS)

            ROUTE = {3: (0, 1, 2, 3, 4), 4: (5, 6, 7, 8, 9), 5: (14, 15, 10), 6: (11, 12, 13)}

            def between(b, par, more, k, point):
                js = SWEEP.get(k - 1, ())
                if swept(b, par, more).stop and point in (1, 3) and point // 2 < len(js):
                    gate(b, swept(b, par, more), js[point // 2])
                if k == 13 and not first(b):
                    if point == 0:
                        add_residual(b - 1, 1 - par)
                    if point == 2:
                        add_bias(b - 1, 1 - par)
                if more:
                    if k == 1 and point == 0:
                        norm(b + 1, 1 - par)
                    stages = ROUTE.get(k, ())
                    if point < len(stages):
                        route(b + 1, 1 - par, stages[point])
                    if 7 <= k < 7 + NG and point == 2:
                        rounds(b + 1, k - 7)
                    if 8 <= k < 8 + NG and point == 4:
                        absolutes(b + 1, 1 - par, k - 8)

            def steps(b, par, more):
                for k in range(NH + (0 if more else LAG)):
                    lb, g, there = lagged(b, k, LAG)
                    lpar = par if k >= LAG else 1 - par
                    if there:
                        invert(lb, g)
                    if k < NH:
                        negate(b, k, 0)
                    if there:
                        weigh(lb, g, lpar)
                    if k < NH:
                        negate(b, k, 1)
                        between(b, par, more, k, 0)
                        negate(b, k, 2)
                        between(b, par, more, k, 1)
                        for rb, hp, what in rotated(b, k, more):
                            rotate(rb, hp, what)
                        between(b, par, more, k, 2)
                    if there and more and k in LOW_BY_VECTOR:
                        scale_low(lb, g)
                    if k < NH:
                        between(b, par, more, k, 3)
                    if there:
                        combine(lb, g)
                    if k < NH:
                        between(b, par, more, k, 4)

            body(dve, steps, prologue)
            add_residual(B - 1, (B - 1) % 2)
            add_bias(B - 1, (B - 1) % 2)

        @block.gpsimd
        def _(pool):
            tt = nc.gpsimd.tensor_tensor

            def part_turns(nb, par, t):
                pool.wait_ge(whole_made, NG * nb + t + 1)
                wait(pool, k_prod, HP * (nb - 1))
                tt(cs[:, par, t, 1, :], turns[:, t % 2], whole[:, :], ALU.subtract).then_inc(frac_made, 1)

            def add_rotated(b, hp, what):
                H, r = b * HP + hp, hp % 2
                wait(pool, qk_in[r], 64 * (b * (HP // 2) + hp // 2))
                if what == 1:
                    pool.wait_ge(k_sin, H + 1)
                pool.wait_ge((q_prod, k_prod)[what], H + 1)
                tt(rot[:, r, what], prod[:, what, 0], prod[:, what, 1], ALU.add).then_inc(rot_made, 1)

            def multiply_k_half(b, hp):
                H = b * HP + hp
                pool.wait_ge(k_kept, b * (HP // 2) + hp // 2 + 1)
                pool.wait_ge(pair_cs_in[hp % 2], 64 * (b * (HP // 2) + hp // 2 + 1))
                wait(pool, rot_made, 2 * H)
                tt(prod[:, 1, 1].rearrange("p (s i) -> p s i", s=2),
                   k_half[:, :].rearrange("p (o i) -> p o i", o=1).broadcast_to([128, 2, N]),
                   pair_cs[:, hp % 2, 1].rearrange("p (s i) -> p s i", s=2), ALU.mult).then_inc(k_sin, 1)

            def add_slots(b, g):
                G, r = b * NH + g, g % 2
                pool.wait_ge(exp_made, 3 * G + 1)
                wait(pool, probs_made, G - RING + 1)
                e = expd[:, r, 0].rearrange("p (s t j) -> p s t j", s=2, t=2)
                tt(sums[:, g % RING, 0:256].rearrange("p (s j) -> p s j", s=2), e[:, :, 0], e[:, :, 1], ALU.add).then_inc(slots_added, 1)
                pool.wait_ge(exp_made, 3 * G + 3)
                tt(sums[:, g % RING, 256:768].rearrange("p (s j) -> p s j", s=2), expd[:, r, 1:3, 0:256], expd[:, r, 1:3, 256:512],
                   ALU.add).then_inc(slots_added, 1)

            def prologue():
                nc.gpsimd.memset(wout_sb[:, :, :], 0.0).then_inc(zeroed, 1)
                nc.gpsimd.memset(qk[:, :, :, :, :], 0.0).then_inc(zeroed, 1)
                pool.wait_ge(weights_in, 16 * WEIGHT_LOADS)
                halves = lambda t: t.rearrange("p (h c f) -> p h c f", c=2, f=F)
                q_from, q_to = halves(wq_sb[:, :]), halves(wq_rot[:, :])
                nc.gpsimd.tensor_scalar(q_to[:, :, 0], q_from[:, :, 1], -1.0, None, ALU.mult).then_inc(weights_made, 1)
                nc.gpsimd.tensor_copy(q_to[:, :, 1], q_from[:, :, 0]).then_inc(weights_made, 1)
                k_from = halves(wk_in)
                both = lambda v: v.rearrange("p h (o f) -> p h o f", o=1).broadcast_to([128, NKV, 2, v.shape[-1]])
                nc.gpsimd.tensor_copy(wk_two[:, :, :, :], both(wk_in.rearrange("p (h d) -> p h d", h=NKV))).then_inc(weights_made, 1)
                nc.gpsimd.tensor_scalar(wk_rot[:, :, :, 0:F], both(k_from[:, :, 1]), -1.0, None, ALU.mult).then_inc(weights_made, 1)
                nc.gpsimd.tensor_copy(wk_rot[:, :, :, F:D], both(k_from[:, :, 0])).then_inc(weights_made, 1)
                for t in range(NG):
                    part_turns(0, 0, t)
                for hp in range(2):
                    multiply_k_half(0, hp)
                    add_rotated(0, hp, 0)
                    add_rotated(0, hp, 1)

            def steps(b, par, more):
                for k in range(NH + (0 if more else 1)):
                    for rb, hp, what in rotated(b, k, more) if k < NH else ():
                        if what == 1:
                            multiply_k_half(rb, hp)
                    if k < NH:
                        for rb, hp, what in rotated(b, k, more):
                            add_rotated(rb, hp, what)
                    lb, g, there = lagged(b, k, 1)
                    if there:
                        add_slots(lb, g)
                    if more and 7 <= k < 7 + NG:
                        part_turns(b + 1, 1 - par, k - 7)

            body(pool, steps, prologue)


_INS = ["L0_attn_x", "L0_attn_wq", "L0_attn_wk", "L0_attn_wv", "L0_attn_wr", "L0_attn_wo", "L0_ffn_Win", "L0_ffn_bin_",
        "L0_ffn_W1", "L0_ffn_b1", "L0_ffn_W2", "L0_ffn_b2", "L0_ffn_Wout", "L0_ffn_bout"]


def kernel(**inputs):
    import numpy as _np
    import concourse.bacc as _bacc
    from concourse import mybir as _mybir
    from concourse.bass_utils import run_bass_kernel_spmd as _run

    nc = _bacc.Bacc("TRN2", target_bir_lowering=False, num_devices=1)
    arrays, args = {}, []
    for name in _INS:
        a = _np.ascontiguousarray(inputs[name])
        arrays[f"in_{name}_dram"] = a
        args.append(nc.dram_tensor(f"in_{name}_dram", a.shape, _mybir.dt.from_np(a.dtype), kind="ExternalInput").ap())
    arrays["shape_constants"] = shape_constants()
    args.append(nc.dram_tensor("shape_constants", (128, C_COLS), _mybir.dt.float32, kind="ExternalInput").ap())
    args.append(nc.dram_tensor("out_0_dram", (B, N, E), _mybir.dt.float32, kind="ExternalOutput").ap())
    routed_attention_block(nc, *args)
    r = _run(nc, [arrays], core_ids=[0])
    return r.results[0]["out_0_dram"]
```
